# Optimizing a Trainium2 kernel written in Bass

```python
import numpy as np
import jax
import jax.numpy as jnp

def _softmax(x, axis=-1):
    return jax.nn.softmax(x, axis=axis)

def _gelu(x):
    return jax.nn.gelu(x, approximate=True)

def _silu(x):
    return jax.nn.silu(x)

def _sigmoid(x):
    return jax.nn.sigmoid(x)

def _layernorm(x, axis=-1, eps=1e-05):
    m = jnp.mean(x, axis=axis, keepdims=True)
    v = jnp.var(x, axis=axis, keepdims=True)
    return (x - m) / jnp.sqrt(v + eps)

def _scatter_add(tgt, idx, src, axis=0):
    return tgt.at[idx].add(src)

def _segment_sum(src, seg, n):
    return jax.ops.segment_sum(src, seg, n)
kernel_name = 'mk_gnn_preln_d4_gnn_r32_deba0b'

def setup_inputs(seed: int=0):
    np.random.seed(seed)
    _w = jnp.asarray

    def _rec_inputs():
        import jax
        import jax.numpy as jnp
        _gk = jax.random.key(seed)
        x = -0.0005121 + 1.001 * jax.random.normal(jax.random.fold_in(_gk, 1), (3125, 64), jnp.float32)
        _s = jax.random.randint(jax.random.fold_in(_gk, 2), (50000,), 0, 3125, jnp.int32)
        _d = jax.random.randint(jax.random.fold_in(_gk, 3), (50000,), 0, 3125, jnp.int32)
        _loop = jnp.arange(3125, dtype=jnp.int32)
        src = jnp.concatenate([_s, _d, _loop])
        dst = jnp.concatenate([_d, _s, _loop])
        _o = jnp.argsort(dst, stable=True)
        src = src[_o]
        dst = dst[_o]
        edge_attr_16 = 6.40344e-05 + 1.00026 * jax.random.normal(jax.random.fold_in(_gk, 12), (103125, 16), jnp.float32)
        edge_attr_3 = -0.000451519 + 1.00018 * jax.random.normal(jax.random.fold_in(_gk, 13), (103125, 3), jnp.float32)
        return (x, src, dst, edge_attr_16, edge_attr_3)
    x, src, dst, edge_attr_16, edge_attr_3 = _rec_inputs()

    def _L0_gnn_setup():
        import jax, jax.numpy as jnp
        import numpy as np
        N, E, IN, H, EC = (50000, 25000, 64, 64, 16)
        CAT = 2 * IN + EC

        def _mp_layer(x, src_f, dst_f, ea_f, W, b):
            n = x.shape[0]
            m = jnp.concatenate([x[dst_f], x[src_f], ea_f], axis=1) @ W.T + b
            agg = jax.ops.segment_sum(m, dst_f, num_segments=n)
            return jax.nn.relu(agg)

        def _batchnorm(x, gamma, beta, eps=1e-05):
            mu = x.mean(axis=0)
            var = x.var(axis=0)
            return (x - mu) * jax.lax.rsqrt(var + eps) * gamma + beta
        key = jax.random.key(seed)
        ks = jax.random.split(key, 8)
        s = 1.0 / np.sqrt(CAT)
        return {'x': jax.random.normal(ks[0], (N, IN), jnp.float32), 'edge_src': jax.random.randint(ks[1], (E,), 0, N, jnp.int32), 'edge_dst': jax.random.randint(ks[2], (E,), 0, N, jnp.int32), 'edge_attr': jax.random.normal(ks[3], (E, EC), jnp.float32), 'W0': jax.random.normal(ks[4], (H, CAT), jnp.float32) * s, 'b0': jnp.zeros((H,), jnp.float32), 'W1': jax.random.normal(ks[5], (H, CAT), jnp.float32) * s, 'b1': jnp.zeros((H,), jnp.float32), 'W2': jax.random.normal(ks[6], (H, CAT), jnp.float32) * s, 'b2': jnp.zeros((H,), jnp.float32), 'g0': jnp.ones((H,), jnp.float32), 'be0': jnp.zeros((H,), jnp.float32), 'g1': jnp.ones((H,), jnp.float32), 'be1': jnp.zeros((H,), jnp.float32)}
    _L0_gnn_all = _L0_gnn_setup()
    _L0_gnn_in = {k: v for k, v in _L0_gnn_all.items() if k in ('W0', 'b0', 'W1', 'b1', 'W2', 'b2', 'g0', 'be0', 'g1', 'be1')}
    del _L0_gnn_all

    def _L1_gnn_setup():
        import jax, jax.numpy as jnp
        import numpy as np
        N_NODES = 50000
        N_EDGES = 25000
        IN_FEAT = 64
        INTER_DIM = 64
        OUT_FEAT = 64
        key = jax.random.key(seed)
        k = jax.random.split(key, 6)
        h = jax.random.normal(k[0], (N_NODES, IN_FEAT), dtype=jnp.float32)
        w = jax.random.normal(k[1], (N_EDGES, 3), dtype=jnp.float32)
        src = jax.random.randint(k[2], (N_EDGES,), 0, N_NODES, dtype=jnp.int32)
        dst = jax.random.randint(k[3], (N_EDGES,), 0, N_NODES, dtype=jnp.int32)
        W1 = jax.random.normal(k[4], (IN_FEAT + 3, INTER_DIM), dtype=jnp.float32) * np.sqrt(2.0 / (IN_FEAT + 3 + INTER_DIM)).astype(np.float32)
        b1 = jnp.zeros((INTER_DIM,), dtype=jnp.float32)
        W2 = jax.random.normal(k[5], (IN_FEAT + INTER_DIM, OUT_FEAT), dtype=jnp.float32) * np.sqrt(2.0 / (IN_FEAT + INTER_DIM + OUT_FEAT)).astype(np.float32)
        return {'h': h, 'w': w, 'src': src, 'dst': dst, 'W1': W1, 'b1': b1, 'W2': W2}
    _L1_gnn_all = _L1_gnn_setup()
    _L1_gnn_in = {k: v for k, v in _L1_gnn_all.items() if k in ('W1', 'b1', 'W2')}
    del _L1_gnn_all

    def _L2_gnn_setup():
        import jax, jax.numpy as jnp
        import numpy as np
        N_NODES = 3125
        N_EDGES = 37500
        D_FEAT = 64
        key = jax.random.key(seed)
        k1, k2, k3 = jax.random.split(key, 3)
        node_f = jax.random.normal(k1, (N_NODES, D_FEAT), dtype=jnp.float32)
        src = jax.random.randint(k2, (N_EDGES,), 0, N_NODES, dtype=jnp.int32)
        dst = jax.random.randint(k3, (N_EDGES,), 0, N_NODES, dtype=jnp.int32)
        return {'node_f': node_f, 'src': src, 'dst': dst}
    _L2_gnn_all = _L2_gnn_setup()
    _L2_gnn_in = {k: v for k, v in _L2_gnn_all.items() if k in ()}
    del _L2_gnn_all

    def _L3_gnn_setup():
        import jax, jax.numpy as jnp
        import numpy as np
        N_NODES = 50000
        N_EDGES = 1250000
        D_FEAT = 64
        key = jax.random.key(seed)
        k1, k2, k3 = jax.random.split(key, 3)
        graph_embedding = jax.random.normal(k1, (N_NODES, D_FEAT), dtype=jnp.float32)
        src = jax.random.randint(k2, (N_EDGES,), 0, N_NODES, dtype=jnp.int64)
        dst = jax.random.randint(k3, (N_EDGES,), 0, N_NODES, dtype=jnp.int64)
        return {'graph_embedding': graph_embedding, 'src': src, 'dst': dst}
    _L3_gnn_all = _L3_gnn_setup()
    _L3_gnn_in = {k: v for k, v in _L3_gnn_all.items() if k in ()}
    del _L3_gnn_all
    return {'x': x, 'src': src, 'dst': dst, 'edge_attr_16': edge_attr_16, 'edge_attr_3': edge_attr_3, 'L0_gnn_W0': _L0_gnn_in['W0'], 'L0_gnn_b0': _L0_gnn_in['b0'], 'L0_gnn_W1': _L0_gnn_in['W1'], 'L0_gnn_b1': _L0_gnn_in['b1'], 'L0_gnn_W2': _L0_gnn_in['W2'], 'L0_gnn_b2': _L0_gnn_in['b2'], 'L0_gnn_g0': _L0_gnn_in['g0'], 'L0_gnn_be0': _L0_gnn_in['be0'], 'L0_gnn_g1': _L0_gnn_in['g1'], 'L0_gnn_be1': _L0_gnn_in['be1'], 'L1_gnn_W1': _L1_gnn_in['W1'], 'L1_gnn_b1': _L1_gnn_in['b1'], 'L1_gnn_W2': _L1_gnn_in['W2']}

def reference(x, src, dst, edge_attr_16, edge_attr_3, L0_gnn_W0, L0_gnn_b0, L0_gnn_W1, L0_gnn_b1, L0_gnn_W2, L0_gnn_b2, L0_gnn_g0, L0_gnn_be0, L0_gnn_g1, L0_gnn_be1, L1_gnn_W1, L1_gnn_b1, L1_gnn_W2):
    import jax
    import jax.numpy as jnp

    def _L0_gnn_ref(x, edge_src, edge_dst, edge_attr, W0, b0, W1, b1, W2, b2, g0, be0, g1, be1):
        import jax, jax.numpy as jnp
        import numpy as np
        N, E, IN, H, EC = (50000, 25000, 64, 64, 16)
        CAT = 2 * IN + EC

        def _mp_layer(x, src_f, dst_f, ea_f, W, b):
            n = x.shape[0]
            m = jnp.concatenate([x[dst_f], x[src_f], ea_f], axis=1) @ W.T + b
            agg = jax.ops.segment_sum(m, dst_f, num_segments=n)
            return jax.nn.relu(agg)

        def _batchnorm(x, gamma, beta, eps=1e-05):
            mu = x.mean(axis=0)
            var = x.var(axis=0)
            return (x - mu) * jax.lax.rsqrt(var + eps) * gamma + beta
        n = x.shape[0]
        loop = jnp.arange(n, dtype=edge_src.dtype)
        src_f = jnp.concatenate([edge_src, loop])
        dst_f = jnp.concatenate([edge_dst, loop])
        ea_f = jnp.concatenate([edge_attr, jnp.ones((n, edge_attr.shape[1]), edge_attr.dtype)], axis=0)
        h = _mp_layer(x, src_f, dst_f, ea_f, W0, b0)
        h = jax.nn.relu(_batchnorm(h, g0, be0))
        h = _mp_layer(h, src_f, dst_f, ea_f, W1, b1)
        h = jax.nn.relu(_batchnorm(h, g1, be1))
        h = _mp_layer(h, src_f, dst_f, ea_f, W2, b2)
        return h

    def _L1_gnn_ref(h, w, src, dst, W1, b1, W2):
        import jax, jax.numpy as jnp
        import numpy as np
        N_NODES = 50000
        N_EDGES = 25000
        IN_FEAT = 64
        INTER_DIM = 64
        OUT_FEAT = 64
        m = jnp.concatenate([h[src], w], axis=1)
        tmp = jax.nn.relu(m @ W1 + b1)
        h_N = jax.ops.segment_sum(tmp, dst, num_segments=h.shape[0])
        h_total = jnp.concatenate([h, h_N], axis=1)
        return jax.nn.relu(h_total @ W2)

    def _L2_gnn_ref(node_f, src, dst):
        import jax, jax.numpy as jnp
        import numpy as np
        N_NODES = 3125
        N_EDGES = 37500
        D_FEAT = 64
        N = node_f.shape[0]
        ones = jnp.ones(src.shape, dtype=node_f.dtype)
        deg_out = jax.ops.segment_sum(ones, src, num_segments=N)
        norm_out = jnp.clip(deg_out, 1.0, None) ** (-0.5)
        h = node_f * norm_out[:, None]
        agg = jax.ops.segment_sum(h[src], dst, num_segments=N)
        deg_in = jax.ops.segment_sum(ones, dst, num_segments=N)
        norm_in = jnp.clip(deg_in, 1.0, None) ** (-0.5)
        return agg * norm_in[:, None]

    def _L3_gnn_ref(graph_embedding, src, dst):
        import jax, jax.numpy as jnp
        import numpy as np
        N_NODES = 50000
        N_EDGES = 1250000
        D_FEAT = 64
        messages = graph_embedding[src]
        out = jax.ops.segment_sum(messages, dst, num_segments=graph_embedding.shape[0])
        return out
    h = jnp.maximum(_layernorm(x, axis=-1), 0.0)
    x = x + _L0_gnn_ref(h, src, dst, edge_attr_16, L0_gnn_W0, L0_gnn_b0, L0_gnn_W1, L0_gnn_b1, L0_gnn_W2, L0_gnn_b2, L0_gnn_g0, L0_gnn_be0, L0_gnn_g1, L0_gnn_be1)
    h = jnp.maximum(_layernorm(x, axis=-1), 0.0)
    x = x + _L1_gnn_ref(h, edge_attr_3, src, dst, L1_gnn_W1, L1_gnn_b1, L1_gnn_W2)
    h = jnp.maximum(_layernorm(x, axis=-1), 0.0)
    x = x + _L2_gnn_ref(h, src, dst)
    h = jnp.maximum(_layernorm(x, axis=-1), 0.0)
    x = x + _L3_gnn_ref(h, src, dst)
    return x

_drawn_inputs = setup_inputs


def setup_inputs(seed=0):
    import zlib

    import numpy as np

    out = dict(_drawn_inputs(seed))
    spreads = {'L0_gnn_b0': (0.0, 0.1),
     'L0_gnn_b1': (0.0, 0.1),
     'L0_gnn_b2': (0.0, 0.1),
     'L0_gnn_g0': (1.0, 0.2),
     'L0_gnn_be0': (0.0, 0.287),
     'L0_gnn_g1': (1.0, 0.2),
     'L0_gnn_be1': (0.0, 0.1),
     'L1_gnn_b1': (0.0, 0.1)}
    factors = {'edge_attr_3': 4.498}
    for name, (base, spread) in spreads.items():
        noise = np.random.default_rng([zlib.crc32(name.encode()), seed]).standard_normal(out[name].shape)
        drawn = base * np.exp(spread * noise) if base else spread * noise
        out[name] = jnp.asarray(drawn.astype(out[name].dtype))
    for name, factor in factors.items():
        out[name] = (out[name] * factor).astype(out[name].dtype)
    return out
```

```python
from contextlib import ExitStack

import concourse.bass as bass
from concourse import mybir

F32 = mybir.dt.float32
BF16 = mybir.dt.bfloat16
F16 = mybir.dt.float16
I32 = mybir.dt.int32
I16 = mybir.dt.int16
ALU = mybir.AluOpType
ACT = mybir.ActivationFunctionType
X = mybir.AxisListType.X
ds = bass.ds

N, E, D = 3125, 103125, 64
P = 125
NB = N // P
NC = E // P
EF = 16
EX = EF + 1
CT, CP = 15, 55
HALF = 9
W = 20
NW = -(-N // W)
WK = W * NB
DP = NW * W
WP = 79
G, U = 5, 3
T = NC // (G * U)
RING = 4
EPS = 1e-5
LANES = ((0, 112), (112, P))
SPLIT = ((0, 0, HALF), (1, HALF, CT))


class Chain:

    def __init__(self, engine, sem):
        self.engine, self.sem, self.base, self.t, self.per, self.steps = engine, sem, 0, None, 0, 0

    def link(self, instruction):
        instruction.then_inc(self.sem, 1)
        self.steps += 1
        done = self.base + self.steps
        self.engine.wait_ge(self.sem, done if self.t is None else self.t * self.per + done)

    def enter(self, t, per):
        self.base, self.t, self.per, self.steps = self.base + self.steps, t, per, 0

    def leave(self, trips):
        assert self.steps == self.per, (self.steps, self.per)
        self.base, self.t, self.steps = self.base + trips * self.per, None, 0


def build(nc, x, src, dst, ea16, ea3, w0, b0, w1, b1, w2, b2, g0, be0, g1, be1, mw1, mb1, mw2, out):
    with ExitStack() as ctx:
        ctx.enter_context(nc.allow_non_contiguous_dma(reason="bias columns"))

        def sb(name, shape, dt):
            return ctx.enter_context(nc.sbuf_tensor(name, shape, dt))

        def sem(name):
            return ctx.enter_context(nc.semaphore(name))

        AT = sb("AT", [P, NB * DP], BF16)
        at3 = AT[:, :].rearrange("p (b d) -> p b d", b=NB)
        dstf = sb("dstf", [P, NC], F32)
        srci = sb("srci", [128, NC + G], I32)
        ident = sb("ident", [128, 128], F32)
        ones = sb("ones", [128, P], F32)
        tabs = sb("tabs", [P, P], F16)
        nbj = sb("nbj", [P, NB], F32)
        Wcat = sb("Wcat", [128, 3, D], F32)
        Wex = sb("Wex", [EX, 3, D], F32)
        W1a = sb("W1a", [D, D], F32)
        W2s = sb("W2s", [128, D], F32)
        rows = sb("rows", [P, 5, D], F32)
        ean = sb("ean", [P, NB, EX], F32)
        schedj = sb("schedj", [1, NC, 2], I16)
        stat = sb("stat", [P, 4, D], F32)
        node = sb("node", [P, 6, NB], F32)
        ysum = sb("ysum", [P, D], F32)
        outdeg4 = sb("outdeg4", [P, NB, 4], F32)
        ARENA = 9180
        arena = sb("arena", [128, ARENA], F32)
        psum = ctx.enter_context(nc.psum_tensor("psum", [128, 8, 512], F32))
        mean_n, var_n, indeg1, norm_in, norm_out, tmp_n = (node[:, i, :] for i in range(6))
        fsum, fsq, scale_f, tmp_f = (stat[:, i, :] for i in range(4))

        def area(at, size, p=P):
            assert at + size <= ARENA, (at, size)
            return arena[0:p, at:at + size]

        BLK = NB * D
        X_ = area(0, BLK).rearrange("p (j f) -> p j f", j=NB)
        H_ = area(BLK, BLK).rearrange("p (j f) -> p j f", j=NB)
        R_ = area(2 * BLK, BLK).rearrange("p (j f) -> p j f", j=NB)
        zs = area(3 * BLK, 3 * BLK // 2).bitcast(BF16).rearrange("p (j k f) -> p j k f", j=NB, k=3)
        SQ = area(3 * BLK, BLK).rearrange("p (j f) -> p j f", j=NB)
        cat_at = 3 * BLK + 3 * BLK // 2
        cat = area(cat_at, G * 128).rearrange("p (i f) -> p i f", i=G)
        rz = area(cat_at, G * D).rearrange("p (i f) -> p i f", i=G)
        eac = area(cat_at + 640, G * EX).rearrange("p (i f) -> p i f", i=G)
        catT = area(cat_at + 725, G * P, 128).rearrange("p (i f) -> p i f", i=G)
        junk = area(cat_at + 725, G * P).bitcast(BF16)
        eacT = area(cat_at + 1350, G * P, EX).rearrange("p (i f) -> p i f", i=G)
        key = area(0, NC)
        srcq = area(NC, NC)
        tabk = area(1650, WK // 2).bitcast(F16)
        nbw = area(1900, NW)
        ohk = area(2060, RING * WK // 2).bitcast(BF16)
        ohs = area(3060, RING * 128 // 2).bitcast(BF16)
        schedw = area(3316, 3 * NW // 2 + 1, 1).bitcast(I16)
        zeros = area(3552, 256).bitcast(BF16)
        oh = area(3810, U * G * P).rearrange("p (i d) -> p i d", i=U * G)
        ohx = area(5685, P)
        msg = area(5810, U * G * D, 128).rearrange("p (i f) -> p i f", i=U * G)
        ea3s = area(6770, U * 3 * P, G).rearrange("p (i e k) -> p i e k", i=U, e=P)
        ea3w = area(7895, 3 * G * D, G).rearrange("p (k i f) -> p k i f", k=3, i=G)
        ring = area(8855, U * G, 128).bitcast(I32)
        zidx = area(8870, G, 128).bitcast(I32)
        atf = AT[:, :].bitcast(F32)

        def early(at, size, p=P):
            return atf[0:p, at:at + size]

        dnat = early(0, CT * P, CP).bitcast(I32).rearrange("p (t e) -> p t e", t=CT)
        snat = early(1875, CT * P, CP).bitcast(I32).rearrange("p (t e) -> p t e", t=CT)
        dnf = early(3750, CT * P, CP).rearrange("p (t e) -> p t e", t=CT)
        diag = early(5625, 2 * NC, CP).rearrange("p (k t r) -> p k t r", k=2, t=CT)
        m1, m2, m3 = early(7275, NC, WP), early(8100, NC, WP), early(8925, NC, WP)
        up = early(9750, NC, WP)
        down = early(10575, NC, WP)
        qf = early(11400, NC)
        qi = early(12225, NC).bitcast(I32)
        rf = early(13050, NC)
        eaT = early(14000, NC * EX).rearrange("p (c f) -> p c f", c=NC)
        eas = early(28030, U * P * EF, CP).rearrange("p (i e f) -> p i e f", i=U, f=EF)
        cmpj = early(34100, CT * (NB - 1), CP).rearrange("p (t j) -> p t j", t=CT)
        jtab = early(34500, NB - 1, CP)
        wlo, whi = early(34530, 2, WP), early(34532, 2, WP)
        dmm = early(34540, 2 * CT, CP).rearrange("p (k t) -> p k t", k=2)
        jmm = early(34570, 2 * CT, CP).rearrange("p (k t) -> p k t", k=2)
        wm = early(34600, 6, WP)
        srcf = early(34700, NC)
        snf = early(36000, CT * P, CP).rearrange("p (t e) -> p t e", t=CT)
        wraw = early(38000, 3 * 145, D).rearrange("p (l f) -> p l f", l=3)

        src_v = src.rearrange("(t r e) -> r t e", t=CT, r=CP)
        dst_v = dst.rearrange("(t r e) -> r t e", t=CT, r=CP)
        ea16_v = ea16.rearrange("(c e) f -> c e f", e=P)
        ea3_v = ea3.rearrange("(c e) k -> c e k", e=P)
        x_v = x.rearrange("(j q) f -> q j f", q=P)
        out_v = out.rearrange("(j q) f -> q j f", q=P)
        msgsrc = nc.dram_tensor("msgsrc", (N, D), F32).ap()
        msgsrc_v = msgsrc.rearrange("(j q) f -> q j f", q=P)

        phase_left = sem("phase_left")
        idx_in, w_in, x_in, x_again, ea3w_in = (sem(n) for n in ("idx_in", "w_in", "x_in", "x_again", "ea3w_in"))
        ea_in = [sem(f"ea_in{i}") for i in range(U)]
        ea3_in = [sem(f"ea3_in{i}") for i in range(U)]
        gathered = [sem(f"gathered{i}") for i in range(U)]
        tables, dve_step, act_step = sem("tables"), sem("dve_step"), sem("act_step")
        idx_f32, idx_T, idx_copied = sem("idx_f32"), sem("idx_T"), sem("idx_copied")
        diag_ready, diag_sum, sums_read = sem("diag_ready"), sem("diag_sum"), sem("sums_read")
        win_ready, win_T, w_T = sem("win_ready"), sem("win_T"), sem("w_T")
        ea_T, ea_half_act, ea_half_dve = sem("ea_T"), sem("ea_half_act"), sem("ea_half_dve")
        acc_zeroed, oh_ready, oh_used = sem("acc_zeroed"), sem("oh_ready"), sem("oh_used")
        ohx_ready, ohx_used, zeros_ready = sem("ohx_ready"), sem("ohx_used"), sem("zeros_ready")
        pair_ready, pair_used, window_kept = sem("pair_ready"), sem("pair_used"), sem("window_kept")
        cat_ready, cat_T, catT_ready = sem("cat_ready"), sem("cat_T"), sem("catT_ready")
        prod_ready, prod_read, z1_ready = sem("prod_ready"), sem("prod_read"), sem("z1_ready")
        y_ready, y_free, zs_ready = sem("y_ready"), sem("y_free"), sem("zs_ready")
        fsum_ready, fsum_total, var_ready, std_ready = sem("fsum_ready"), sem("fsum_total"), sem("var_ready"), sem("std_ready")
        outdeg_ready, rows_ready, rows_out, out_done = sem("outdeg_ready"), sem("rows_ready"), sem("rows_out"), sem("out_done")
        ring_ready, ew_ready, premsg_ready, msg_ready = sem("ring_ready"), sem("ew_ready"), sem("premsg_ready"), sem("msg_ready")

        block = ctx.enter_context(nc.Block())
        NTAB = 14
        NWIN = 12 + 2 + 5

        def leave(eng, n):
            eng.drain().then_inc(phase_left, 1)
            eng.wait_ge(phase_left, 5 * n)

        def bank(b, cols, p=P):
            return psum[0:p, b, 0:cols]

        @block.sync
        def _(sp):
            sp.dma_start(dnat, dst_v).then_inc(idx_in, 16)
            sp.dma_start(snat, src_v).then_inc(idx_in, 16)
            for l, (w, b) in enumerate(((w0, b0), (w1, b1), (w2, b2))):
                sp.dma_start(wraw[:, l, 0:D], w[:, D:2 * D]).then_inc(w_in, 16)
                sp.dma_start(wraw[:, l, D:2 * D], w[:, 0:D]).then_inc(w_in, 16)
                sp.dma_start(wraw[:, l, 2 * D:2 * D + EF], w[:, 2 * D:2 * D + EF]).then_inc(w_in, 16)
                sp.dma_start(wraw[:, l, 2 * D + EF:2 * D + EX], b.rearrange("(f a) -> f a", a=1)).then_inc(w_in, 16)
            sp.dma_start(W1a[:, :], mw1[0:D, :]).then_inc(w_in, 16)
            sp.dma_start(W2s[:, :], mw2[:, :]).then_inc(w_in, 16)
            for k, r in enumerate((g0, be0, g1, be1, mb1)):
                sp.dma_start(rows[:, k, :], r.rearrange("(a f) -> a f", a=1).to_broadcast([P, D])).then_inc(w_in, 16)
            with sp.Fori(0, CT // U) as t:
                for u in range(U):
                    sp.wait_ge(ea_half_act, t * U + (u + 1))
                    sp.wait_ge(ea_half_dve, t * U + (u + 1))
                    sp.dma_start(eas[:, u, :, :], ea16_v[ds((t * U + u) * CP, CP)]).then_inc(ea_in[u], 16)
            leave(sp, 1)
            leave(sp, 2)
            leave(sp, 3)
            for a, b in LANES:
                sp.dma_start(R_[a:b], x_v[a:b]).then_inc(x_in, 16)
            for a, b in LANES:
                sp.dma_start(X_[a:b], x_v[a:b]).then_inc(x_again, 16)
            leave(sp, 4)
            sp.wait_ge(rows_ready, 1)
            for a, b in LANES:
                sp.dma_start(msgsrc_v[a:b], R_[a:b]).then_inc(rows_out, 16)
            sp.wait_ge(rows_out, 16 * len(LANES))
            leave(sp, 5)
            sp.wait_ge(zeros_ready, 2)
            for i in range(G):
                sp.dma_start(ea3w[i:i + 1, :, i, :], mw1[D:D + 3, :].rearrange("(a k) f -> a k f", a=1)).then_inc(ea3w_in, 16)
            with sp.Fori(0, T) as t:
                for u in range(U):
                    sp.wait_ge(oh_used, t * (U * G) + (NC + G * u + G))
                    sp.dma_start(ea3s[:, u, :, :], ea3_v[ds((t * U + u) * G, G)]).then_inc(ea3_in[u], 16)
            for n in range(6, 10):
                leave(sp, n)
            for a, b in LANES:
                sp.dma_start(out_v[a:b], X_[a:b]).then_inc(out_done, 16)
            sp.wait_ge(out_done, 16 * len(LANES))

        @block.gpsimd
        def _(pool):
            g = nc.gpsimd
            loose = dict(allow_small_or_imprecise_dtypes=True)
            g.memset(ident[:, :], 0.0).then_inc(tables, 1)
            g.memset(ones[:, :], 1.0).then_inc(tables, 1)
            g.iota(tabs[:, :], pattern=[[1, P]], base=0, channel_multiplier=0, **loose).then_inc(tables, 1)
            g.iota(nbj[:, :], pattern=[[-P, NB]], base=0, channel_multiplier=0, **loose).then_inc(tables, 1)
            g.iota(tabk, pattern=[[1, NB], [NB, W]], base=0, channel_multiplier=0, **loose).then_inc(tables, 1)
            g.iota(nbw, pattern=[[-WK, NW]], base=0, channel_multiplier=0, **loose).then_inc(tables, 1)
            g.iota(up, pattern=[[1, NC]], base=1, channel_multiplier=0, **loose).then_inc(tables, 1)
            g.iota(down, pattern=[[-1, NC]], base=NC, channel_multiplier=0, **loose).then_inc(tables, 1)
            g.iota(jtab, pattern=[[P, NB - 1]], base=P, channel_multiplier=0, **loose).then_inc(tables, 1)
            g.iota(wlo, pattern=[[WP * W, 2]], base=0, channel_multiplier=W, **loose).then_inc(tables, 1)
            g.iota(whi, pattern=[[WP * W, 2]], base=W - 1, channel_multiplier=W, **loose).then_inc(tables, 1)
            g.memset(srci[:, :], 0).then_inc(tables, 1)
            g.memset(zeros, 0.0).then_inc(tables, 1)
            pool.wait_ge(tables, 1)
            g.affine_select(out=ident[:, :], in_=ident[:, :], compare_op=ALU.not_equal, fill=1.0, base=0,
                            pattern=[[-1, 128]], channel_multiplier=1).then_inc(tables, 1)
            g.memset(eaT[:, :, EF:EX], 1.0)
            for n in range(1, 6):
                leave(pool, n)
            g.memset(zidx, 0).then_inc(ring_ready, 1)
            pool.wait_ge(ring_ready, 1)
            g.tensor_tensor(ring[:, 0:G], srci[:, 0:G], zidx, ALU.add).then_inc(ring_ready, 1)
            with pool.Fori(0, T) as t:
                for u in range(U):
                    v = (u + 1) % U
                    pool.wait_ge(oh_used, t * (U * G) + (NC + G * u + 2 * G))
                    pool.wait_ge(ring_ready, t * U + (u + 2))
                    g.tensor_tensor(ring[:, G * v:G * v + G], srci[:, ds((t * U + (u + 1)) * G, G)], zidx,
                                    ALU.add).then_inc(ring_ready, 1)
                    for i in range(G * u, G * u + G):
                        g.indirect_dma_start(msg[:, i, :], None, msgsrc,
                                             bass.IndirectOffsetOnAxis(ring[:, i:i + 1], 0)).then_inc(gathered[u], 16)
            for n in range(6, 10):
                leave(pool, n)

        @block.scalar
        def _(act):
            a = nc.scalar
            chain = Chain(act, act_step)
            act.sem_inc(ea_half_act, U)
            with act.Fori(0, CT // U) as t:
                for u in range(U):
                    act.wait_ge(ea_T, t * U + (u + 1))
                    a.copy(eaT[:, ds((t * U + u) * CP, CP), 0:EF // 2].rearrange("p c f -> p f c"),
                           bank(2 * u, 8 * CP).rearrange("p (f c) -> p f c", f=8)).then_inc(ea_half_act, 1)
            leave(act, 1)
            leave(act, 2)
            act.sem_inc(window_kept, 2)
            with act.register("pairs_done") as pairs:
                act.reg_mov(pairs, RING)
                with act.Fori(0, NW) as w:
                    count = act.value_load(schedw[0:1, ds(3 * w + 2, 1)], min_val=1, max_val=NC)
                    act.reg_add(pairs, pairs, count)
                    act.wait_ge(pair_used, act.snap(pairs, min_val=1, max_val=NC * NW + RING))
                    a.copy(at3[:, :, ds(w * W, W)], psum[0:P, ds((w & 1) + 1, 1), 0:WK].rearrange("p a (b d) -> p (a b) d", d=W)).then_inc(window_kept, 1)
            leave(act, 3)

            def turn(n, nrow, first, with_edges=False):
                act.wait_ge(cat_T, n)
                if with_edges:
                    chain.link(a.copy(eacT[:, 0:4, :], bank(2, 4 * P, EX).rearrange("p (i e) -> p i e", i=4)))
                    chain.link(a.copy(eacT[:, 4, :], bank(3, P, EX)))
                chain.link(a.copy(catT[0:nrow, 0:4, :], bank(first, 4 * P, nrow).rearrange("p (i e) -> p i e", i=4)))
                a.copy(catT[0:nrow, 4, :], bank(first + 1, P, nrow)).then_inc(catT_ready, 1)

            roots = [0]

            def root():
                act.wait_ge(var_ready, roots[0] + 1)
                roots[0] += 1
                return roots[0]

            def node_root():
                root()
                a.activation(tmp_n, var_n, ACT.Sqrt).then_inc(std_ready, 1)

            node_root()
            for l in range(3):
                with act.Fori(0, G) as gg:
                    chain.enter(gg, 3)
                    turn(gg + (G * l + 1), 128, 0, True)
                    chain.leave(G)
                    act.wait_ge(prod_ready, gg + (G * l + 1))
                    a.copy(zs[:, ds(gg * G, G), 0, :], bank(4, G * D).rearrange("p (i f) -> p i f", i=G)).then_inc(z1_ready, 1)
                if l == 0:
                    with act.Fori(0, NB) as b:
                        chain.enter(b, 4)
                        for k in range(4):
                            w4 = DP // 4
                            chain.link(a.activation(junk[:, 0:w4], at3[:, ds(b, 1), k * w4:(k + 1) * w4].rearrange("p a d -> p (a d)"),
                                                    ACT.Copy, accum_out=outdeg4[:, ds(b, 1), k:k + 1].rearrange("p a k -> p (a k)")))
                        chain.leave(NB)
                    act.sem_inc(outdeg_ready, 1)
                if l < 2:
                    root()
                    a.activation(tmp_f, fsq, ACT.Sqrt).then_inc(std_ready, 1)
            leave(act, 4)
            node_root()
            with act.Fori(0, G) as gg:
                chain.enter(gg, 1)
                turn(gg + (3 * G + 1), 128, 0)
                chain.leave(G)
            leave(act, 5)
            with act.Fori(0, T) as t:
                for u in range(U):
                    act.wait_ge(premsg_ready, t * U + (u + 1))
                    m = msg[0:P, G * u:G * u + G, :]
                    a.activation(m, m, ACT.Relu).then_inc(msg_ready, 1)
            leave(act, 6)
            with act.Fori(0, G) as gg:
                chain.enter(gg, 1)
                turn(gg + (4 * G + 1), 128, 4)
                chain.leave(G)
            leave(act, 7)
            node_root()
            root()
            chain.link(a.activation(norm_in, norm_in, ACT.Sqrt))
            a.activation(norm_out, norm_out, ACT.Sqrt).then_inc(std_ready, 1)
            leave(act, 8)
            node_root()
            leave(act, 9)

        @block.tensor
        def _(pe):
            mm, tp = nc.tensor.matmul, nc.tensor.transpose
            pe.wait_ge(tables, NTAB)
            for k, nat in enumerate((dnf, snf)):
                pe.wait_ge(idx_f32, k + 1)
                for b, lo, hi in SPLIT:
                    for t in range(lo, hi):
                        last = tp(psum[0:P, 2 * k + b, (t - lo) * CP:(t - lo + 1) * CP], nat[:, t, :], ident[0:CP, 0:CP])
                last.then_inc(idx_T, 1)
            pe.wait_ge(diag_ready, 1)
            for k in range(2):
                for b, lo, hi in SPLIT:
                    last = mm(bank(4 + 2 * k + b, (hi - lo) * CP, WP), ones[0:CP, 0:WP],
                              diag[:, k, lo:hi, :].rearrange("p t r -> p (t r)"), start=True, stop=True)
            last.then_inc(diag_sum, 1)
            pe.wait_ge(idx_copied, 4)
            pe.wait_ge(diag_ready, 2)
            for k in range(2):
                for b, lo, hi in SPLIT:
                    last = mm(bank(2 * k + b, (hi - lo) * CP, 1), ones[0:CP, 0:1],
                              diag[:, k, lo:hi, :].rearrange("p t r -> p (t r)"), start=True, stop=True)
            last.then_inc(diag_sum, 1)
            pe.wait_ge(win_ready, 1)
            for k in range(6):
                last = mm(psum[0:1, 4, k * WP:(k + 1) * WP], wm[:, k:k + 1], ident[0:WP, 0:WP], start=True, stop=True)
            last.then_inc(win_T, 1)
            pe.wait_ge(w_in, 16 * NWIN)
            for l in range(3):
                tp(psum[:, 7, l * D:(l + 1) * D], wraw[:, l, 0:128], ident[0:D, 0:D])
                last = tp(psum[0:EX, 6, l * D:(l + 1) * D], wraw[:, l, 128:128 + EX], ident[0:D, 0:D])
            last.then_inc(w_T, 1)
            pe.wait_ge(sums_read, 3)
            with pe.Fori(0, CT // U) as t:
                for u in range(U):
                    pe.wait_ge(ea_in[u], t * 16 + 16)
                    mm(psum[0:P, 7, 0:1], ones[0:CP, 0:P], ones[0:CP, 0:1], start=True, stop=True)
                    for f in range(EF):
                        last = tp(psum[0:P, 2 * u + f // 8, (f % 8) * CP:(f % 8 + 1) * CP], eas[:, u, :, f], ident[0:CP, 0:CP])
                    last.then_inc(ea_T, 1)
            leave(pe, 1)

            pe.sem_inc(oh_used, U * G)
            pe.sem_inc(ohx_used, 1)
            extra = ctx.enter_context(pe.register("extra_pe"))
            pe.reg_mov(extra, 0)

            def scatter_chunk(n, c, slot, width, place, payload):
                lo = pe.value_load(schedj[0:1, ds(c, 1), 0:1].rearrange("p a b -> p (a b)"), min_val=0, max_val=NB - 1)
                end = pe.value_load(schedj[0:1, ds(c, 1), 1:2].rearrange("p a b -> p (a b)"), min_val=1, max_val=NB)
                with pe.If(end > lo + 1):
                    with pe.Fori(lo + 1, end) as j:
                        pe.reg_add(extra, extra, 1)
                        pe.wait_ge(ohx_ready, pe.snap(extra, min_val=1, max_val=NC * NB))
                        mm(place(j), ohx, payload, start=False, stop=False, skip_group_check=True).then_inc(ohx_used, 1)
                pe.wait_ge(oh_ready, n + 1)
                mm(place(lo), oh[:, slot, :], payload, start=False, stop=False, skip_group_check=True).then_inc(oh_used, 1)

            def zero(banks):
                for b in banks:
                    last = mm(bank(b, 512), zeros[:, 0:P], zeros[:, 0:512], start=True, stop=True)
                return last

            zero([0])
            with pe.Fori(0, T) as t:
                for s in range(U * G):
                    c = t * (U * G) + s
                    scatter_chunk(c, c, s, EX, lambda j: psum[0:P, 0, ds(j * EX, EX)], eaT[:, ds(c, 1), :].rearrange("p a f -> p (a f)"))
            leave(pe, 2)

            pe.sem_inc(pair_used, RING)
            pairs = ctx.enter_context(pe.register("pairs_pe"))
            pe.reg_mov(pairs, 0)
            with pe.Fori(0, NW) as w:
                start = pe.value_load(schedw[0:1, ds(3 * w, 1)], min_val=0, max_val=NC - 1)
                end = pe.value_load(schedw[0:1, ds(3 * w + 1, 1)], min_val=1, max_val=NC)
                pe.wait_ge(window_kept, w + 1)
                half = pe.snap((w & 1) + 1, min_val=1, max_val=2)
                acc = psum[0:P, ds(half, 1), 0:WK].rearrange("p a k -> p (a k)")
                mm(acc, zeros[:, 0:P], zeros[:, 0:WK], start=True, stop=True)
                with pe.Fori(start, end) as c:
                    slot = pe.snap(pe.snap(pairs, min_val=0, max_val=NC * NW) & (RING - 1), min_val=0, max_val=RING - 1)
                    pe.reg_add(pairs, pairs, 1)
                    pe.wait_ge(pair_ready, pe.snap(pairs, min_val=1, max_val=NC * NW))
                    mm(acc, ohs[:, ds(slot * 128, P)], ohk[:, ds(slot * WK, WK)], start=False, stop=False,
                       skip_group_check=True).then_inc(pair_used, 1)
            leave(pe, 3)

            def turn(n, nrow, first, with_edges=False):
                pe.wait_ge(cat_ready, n)
                for i in range(G):
                    if with_edges:
                        tp(psum[0:EX, 2 + i // 4, (i % 4) * P:(i % 4 + 1) * P], eac[:, i, :], ident[0:P, 0:P])
                    last = tp(psum[0:nrow, first + i // 4, (i % 4) * P:(i % 4 + 1) * P], cat[:, i, 0:nrow], ident[0:P, 0:P])
                last.then_inc(cat_T, 1)
                pe.wait_ge(catT_ready, n)

            applied = [0]

            def apply():
                base = NB * applied[0]
                applied[0] += 1
                pe.wait_ge(zs_ready, applied[0])
                with pe.Fori(0, G) as gg:
                    for u in range(G):
                        pe.wait_ge(y_free, gg * G + (base + u + 1))
                        for b in range(NB):
                            last = mm(bank(u, 3 * D), at3[:, b, ds((gg * G + u) * P, P)],
                                      zs[:, b, :, :].rearrange("p k f -> p (k f)"), start=(b == 0), stop=(b == NB - 1))
                        last.then_inc(y_ready, 1)

            totals = [0]

            def total():
                totals[0] += 1
                pe.wait_ge(fsum_ready, totals[0])
                mm(bank(6, D), ones[0:P, 0:P], fsum, start=True, stop=True).then_inc(fsum_total, 1)

            pe.sem_inc(y_free, G)
            for l in range(3):
                with pe.Fori(0, G) as gg:
                    turn(gg + (G * l + 1), 128, 0, True)
                    for i in range(G):
                        mm(psum[0:P, 4, i * D:(i + 1) * D], catT[0:D, i, :], Wcat[0:D, l, :], start=True, stop=True)
                    for i in range(G):
                        o = psum[0:P, 5, i * D:(i + 1) * D]
                        mm(o, catT[:, i, :], Wcat[:, l, :], start=True, stop=False)
                        last = mm(o, eacT[:, i, :], Wex[:, l, :], start=False, stop=True)
                    last.then_inc(prod_ready, 1)
                apply()
                if l < 2:
                    total()
                    total()
            leave(pe, 4)
            with pe.Fori(0, G) as gg:
                turn(gg + (3 * G + 1), 128, 0)
                for i in range(G):
                    last = mm(psum[0:P, 4, i * D:(i + 1) * D], catT[0:D, i, :], W1a[:, :], start=True, stop=True)
                last.then_inc(prod_ready, 1)
            leave(pe, 5)
            pe.wait_ge(zeros_ready, 2)
            zero(range(4))
            pe.wait_ge(ea3w_in, 16 * G)
            with pe.Fori(0, T) as t:
                for u in range(U):
                    pe.wait_ge(ea3_in[u], t * 16 + 16)
                    for k in range(3):
                        last = mm(bank(4 + u, G * D), ea3s[:, u, :, k], ea3w[:, k, :, :].rearrange("p i f -> p (i f)"),
                                  start=(k == 0), stop=(k == 2))
                    last.then_inc(ew_ready, 1)
                    pe.wait_ge(msg_ready, t * U + (u + 1))
                    for i in range(G):
                        s = G * u + i
                        c = t * (U * G) + s
                        scatter_chunk(c + NC, c, s, D,
                                      lambda j: psum[0:P, 0:4, :].rearrange("p b k -> p (b k)")[:, ds(j * D, D)], msg[0:P, s, :])
            leave(pe, 6)
            with pe.Fori(0, G) as gg:
                turn(gg + (4 * G + 1), 128, 4)
                for i in range(G):
                    last = mm(psum[0:P, 6, i * D:(i + 1) * D], catT[:, i, :], W2s[:, :], start=True, stop=True)
                last.then_inc(prod_ready, 1)
            leave(pe, 7)
            apply()
            leave(pe, 8)
            apply()
            leave(pe, 9)

        @block.vector
        def _(dve):
            v = nc.vector
            chain = Chain(dve, dve_step)
            link = chain.link
            dve.sem_inc(ea_half_dve, U)
            dve.wait_ge(idx_in, 32)
            v.tensor_copy(dnf, dnat).then_inc(idx_f32, 1)
            v.tensor_copy(snf, snat).then_inc(idx_f32, 1)
            dve.wait_ge(idx_f32, 1)
            dve.wait_ge(tables, NTAB)
            link(v.tensor_reduce(dmm[:, 0, :], dnf, X, ALU.min))
            link(v.tensor_reduce(dmm[:, 1, :], dnf, X, ALU.max))
            rr = ident[0:CP, 0:CP].unsqueeze(1).to_broadcast([CP, CT, CP])

            def diagonal(vals):
                for k in range(2):
                    link(v.tensor_tensor(diag[:, k, :, :], rr, vals[:, k, :].unsqueeze(2).to_broadcast([CP, CT, CP]), ALU.mult))

            diagonal(dmm)
            dve.sem_inc(diag_ready, 1)
            for k in range(2):
                link(v.tensor_tensor(cmpj, dmm[:, k, :].unsqueeze(2).to_broadcast([CP, CT, NB - 1]),
                                     jtab.unsqueeze(1).to_broadcast([CP, CT, NB - 1]), ALU.is_ge))
                link(v.tensor_reduce(jmm[:, k, :], cmpj, X, ALU.add))
            link(v.tensor_scalar(jmm[:, 1, :], jmm[:, 1, :], 1.0, None, ALU.add))
            for k, col in enumerate((dstf[:, :], srcf)):
                dve.wait_ge(idx_T, k + 1)
                for b, lo, hi in SPLIT:
                    v.tensor_copy(col[:, lo * CP:hi * CP], bank(2 * k + b, (hi - lo) * CP)).then_inc(idx_copied, 1)
            dve.wait_ge(diag_sum, 1)
            diagonal(jmm)
            dve.sem_inc(diag_ready, 1)
            dve.wait_ge(idx_copied, 4)
            v.tensor_copy(srci[0:P, 0:NC], srcf)
            link(v.tensor_scalar(qi, srcf, 1.0 / P, -0.5 + 0.5 / P, ALU.mult, ALU.add))
            link(v.tensor_copy(qf, qi))
            link(v.scalar_tensor_tensor(out=rf, in0=qf, scalar=-float(P), in1=srcf, op0=ALU.mult, op1=ALU.add))
            link(v.scalar_tensor_tensor(out=qf, in0=rf, scalar=float(P), in1=qf, op0=ALU.is_ge, op1=ALU.add))
            link(v.tensor_scalar(rf, rf, 0.0, None, ALU.is_lt))
            link(v.tensor_tensor(qf, qf, rf, ALU.subtract))
            link(v.scalar_tensor_tensor(out=srcq, in0=qf, scalar=-float(P), in1=srcf, op0=ALU.mult, op1=ALU.add))
            link(v.scalar_tensor_tensor(out=key, in0=dstf[:, :], scalar=float(NB), in1=qf, op0=ALU.mult, op1=ALU.add))
            for h in range(2):
                ws, we, wn = (wm[:, 3 * h + k:3 * h + k + 1] for k in range(3))
                for b, lo, hi in SPLIT:
                    s = slice(lo * CP, hi * CP)
                    link(v.tensor_scalar(m1[:, s], bank(4 + b, (hi - lo) * CP, WP), whi[:, h:h + 1], None, ALU.is_le))
                    link(v.scalar_tensor_tensor(out=m2[:, s], in0=bank(6 + b, (hi - lo) * CP, WP), scalar=wlo[:, h:h + 1],
                                                in1=m1[:, s], op0=ALU.is_ge, op1=ALU.mult))
                link(v.tensor_tensor(m3, m2, up, ALU.mult))
                link(v.tensor_reduce(we, m3, X, ALU.max))
                link(v.tensor_tensor(m3, m2, down, ALU.mult))
                link(v.tensor_reduce(ws, m3, X, ALU.max))
                link(v.tensor_scalar(we, we, 1.0, None, ALU.max))
                link(v.tensor_scalar(ws, ws, -1.0, float(NC), ALU.mult, ALU.add))
                link(v.scalar_tensor_tensor(out=ws, in0=we, scalar=-1.0,
                                            in1=ws, op0=ALU.add, op1=ALU.min))
                link(v.tensor_tensor(wn, we, ws, ALU.subtract))
            dve.sem_inc(win_ready, 1)
            dve.wait_ge(diag_sum, 2)
            for k in range(2):
                for b, lo, hi in SPLIT:
                    last = v.tensor_copy(schedj[:, lo * CP:hi * CP, k:k + 1].rearrange("p c a -> p (c a)"), bank(2 * k + b, (hi - lo) * CP, 1))
            last.then_inc(sums_read, 1)
            dve.wait_ge(win_T, 1)
            for h in range(2):
                nw = min(WP, NW - h * WP)
                for k in range(3):
                    last = v.tensor_copy(schedw[:, 3 * h * WP:3 * (h * WP + nw)].rearrange("p (w k) -> p w k", k=3)[:, :, k],
                                         psum[0:1, 4, (3 * h + k) * WP:(3 * h + k) * WP + nw])
            last.then_inc(sums_read, 1)
            dve.wait_ge(w_T, 1)
            link(v.tensor_copy(Wcat[:, :, :], psum[:, 7, 0:3 * D].rearrange("p (l f) -> p l f", l=3)))
            link(v.tensor_copy(Wex[:, :, :], psum[0:EX, 6, 0:3 * D].rearrange("p (l f) -> p l f", l=3)))
            dve.sem_inc(sums_read, 1)
            with dve.Fori(0, CT // U) as t:
                for u in range(U):
                    dve.wait_ge(ea_T, t * U + (u + 1))
                    v.tensor_copy(eaT[:, ds((t * U + u) * CP, CP), EF // 2:EF].rearrange("p c f -> p f c"),
                                  bank(2 * u + 1, 8 * CP).rearrange("p (f c) -> p f c", f=8)).then_inc(ea_half_dve, 1)
            leave(dve, 1)

            extra = ctx.enter_context(dve.register("extra_dve"))
            dve.reg_mov(extra, 0)

            def onehots(n, c, slot):
                lo = dve.value_load(schedj[0:1, ds(c, 1), 0:1].rearrange("p a b -> p (a b)"), min_val=0, max_val=NB - 1)
                end = dve.value_load(schedj[0:1, ds(c, 1), 1:2].rearrange("p a b -> p (a b)"), min_val=1, max_val=NB)
                dve.wait_ge(oh_used, n + 1)
                v.tensor_scalar(oh[:, slot, :], tabs[:, :], dstf[:, ds(c, 1)], nbj[:, ds(lo, 1)], ALU.subtract,
                                ALU.is_equal).then_inc(oh_ready, 1)
                with dve.If(end > lo + 1):
                    with dve.Fori(lo + 1, end) as j:
                        dve.reg_add(extra, extra, 1)
                        dve.wait_ge(ohx_used, dve.snap(extra, min_val=1, max_val=NC * NB))
                        v.tensor_scalar(ohx, tabs[:, :], dstf[:, ds(c, 1)], nbj[:, ds(j, 1)], ALU.subtract,
                                        ALU.is_equal).then_inc(ohx_ready, 1)

            with dve.Fori(0, T) as t:
                for s in range(U * G):
                    c = t * (U * G) + s
                    onehots(c, c, s)
            leave(dve, 2)
            link(v.tensor_scalar(ean[:, :, :], psum[0:P, 0, 0:NB * EX].rearrange("p (j f) -> p j f", j=NB), 1.0, None, ALU.add))

            pairs = ctx.enter_context(dve.register("pairs_dve"))
            dve.reg_mov(pairs, 0)
            with dve.Fori(0, NW) as w:
                start = dve.value_load(schedw[0:1, ds(3 * w, 1)], min_val=0, max_val=NC - 1)
                end = dve.value_load(schedw[0:1, ds(3 * w + 1, 1)], min_val=1, max_val=NC)
                with dve.Fori(start, end) as c:
                    slot = dve.snap(dve.snap(pairs, min_val=0, max_val=NC * NW) & (RING - 1), min_val=0, max_val=RING - 1)
                    dve.reg_add(pairs, pairs, 1)
                    dve.wait_ge(pair_used, dve.snap(pairs, min_val=1, max_val=NC * NW))
                    v.tensor_scalar(ohk[:, ds(slot * WK, WK)], tabk, key[:, ds(c, 1)], nbw[:, ds(w, 1)], ALU.subtract, ALU.is_equal)
                    v.tensor_scalar(ohs[:, ds(slot * 128, P)], tabs[:, :], srcq[:, ds(c, 1)], None, ALU.is_equal).then_inc(pair_ready, 1)
            leave(dve, 3)

            def over_f(a):
                return a.unsqueeze(2).to_broadcast([P, NB, D])

            def over_j(a):
                return a.unsqueeze(1).to_broadcast([P, NB, D])

            roots = [0]

            def std(step):
                step.then_inc(var_ready, 1)
                roots[0] += 1
                dve.wait_ge(std_ready, roots[0])

            def layernorm(x_):
                link(v.tensor_reduce(mean_n, x_, X, ALU.add))
                link(v.tensor_scalar(mean_n, mean_n, 1.0 / D, None, ALU.mult))
                link(v.tensor_tensor(H_, x_, over_f(mean_n), ALU.subtract))
                link(v.tensor_tensor(SQ, H_, H_, ALU.mult))
                link(v.tensor_reduce(var_n, SQ, X, ALU.add))
                std(v.tensor_scalar(var_n, var_n, 1.0 / D, EPS, ALU.mult, ALU.add))
                link(v.reciprocal(tmp_n, tmp_n))
                link(v.scalar_tensor_tensor(out=H_, in0=H_, scalar=0.0, in1=over_f(tmp_n), op0=ALU.max, op1=ALU.mult))

            def split():
                for k in range(3):
                    last = v.tensor_copy(zs[:, :, k, :], H_)
                    if k < 2:
                        link(last)
                        link(v.tensor_tensor(H_, H_, zs[:, :, k, :], ALU.subtract))
                last.then_inc(zs_ready, 1)

            applied = [0]

            def take(per, use):
                base = NB * applied[0]
                applied[0] += 1
                with dve.Fori(0, G) as gg:
                    chain.enter(gg, G * per)
                    for u in range(G):
                        j = gg * G + u
                        dve.wait_ge(y_ready, j + (base + 1))
                        link(v.tensor_reduce(ysum[:, :], bank(u, 3 * D).rearrange("p (k f) -> p f k", k=3), X, ALU.add))
                        use(j)
                        dve.sem_inc(y_free, 1)
                    chain.leave(G)

            def feature_total(step):
                step.then_inc(fsum_ready, 1)
                totals[0] += 1
                dve.wait_ge(fsum_total, totals[0])

            totals = [0]

            def batchnorm(gamma, beta):
                feature_total(v.tensor_reduce(fsum, R_.rearrange("p j f -> p f j"), X, ALU.add))
                link(v.tensor_scalar(scale_f, bank(6, D), 1.0 / N, None, ALU.mult))
                link(v.tensor_tensor(R_, R_, over_j(scale_f), ALU.subtract))
                link(v.tensor_tensor(SQ, R_, R_, ALU.mult))
                feature_total(v.tensor_reduce(fsum, SQ.rearrange("p j f -> p f j"), X, ALU.add))
                std(v.tensor_scalar(fsq, bank(6, D), 1.0 / N, EPS, ALU.mult, ALU.add))
                link(v.reciprocal(tmp_f, tmp_f))
                link(v.tensor_tensor(scale_f, tmp_f, rows[:, gamma, :], ALU.mult))
                link(v.tensor_tensor(R_, R_, over_j(scale_f), ALU.mult))
                link(v.tensor_tensor(R_, R_, over_j(rows[:, beta, :]), ALU.add))
                link(v.tensor_scalar(H_, R_, 0.0, None, ALU.max))

            link(v.tensor_copy(indeg1, ean[:, :, EF:EX].rearrange("p j a -> p (j a)")))
            dve.wait_ge(x_in, 16 * len(LANES))
            layernorm(R_)
            for l in range(3):
                with dve.Fori(0, G) as gg:
                    chain.enter(gg, 6)
                    js = ds(gg * G, G)
                    n = gg + (G * l + 1)
                    link(v.tensor_copy(cat[:, :, 0:D], H_[:, js, :]))
                    link(v.tensor_tensor(cat[:, :, D:2 * D], H_[:, js, :], indeg1[:, js].unsqueeze(2).to_broadcast([P, G, D]), ALU.mult))
                    v.tensor_copy(eac, ean[:, js, :]).then_inc(cat_ready, 1)
                    dve.wait_ge(z1_ready, n)
                    link(v.tensor_tensor(rz, bank(4, G * D).rearrange("p (i f) -> p i f", i=G), zs[:, js, 0, :], ALU.subtract))
                    link(v.tensor_copy(zs[:, js, 1, :], rz))
                    link(v.tensor_tensor(rz, rz, zs[:, js, 1, :], ALU.subtract))
                    link(v.tensor_copy(zs[:, js, 2, :], rz))
                    v.tensor_copy(R_[:, js, :], bank(5, G * D).rearrange("p (i f) -> p i f", i=G)).then_inc(prod_read, 1)
                    dve.wait_ge(prod_read, n)
                    chain.leave(G)
                dve.sem_inc(zs_ready, 1)
                take(2, lambda j: link(v.tensor_tensor(R_[:, ds(j, 1), :], R_[:, ds(j, 1), :], ysum[:, :].unsqueeze(1), ALU.add)))
                link(v.tensor_scalar(R_, R_, 0.0, None, ALU.max))
                if l < 2:
                    batchnorm(2 * l, 2 * l + 1)
            dve.wait_ge(x_again, 16 * len(LANES))
            link(v.tensor_tensor(X_, X_, R_, ALU.add))
            leave(dve, 4)

            layernorm(X_)
            with dve.Fori(0, G) as gg:
                js = ds(gg * G, G)
                v.tensor_copy(cat[:, :, 0:D], H_[:, js, :]).then_inc(cat_ready, 1)
                dve.wait_ge(prod_ready, gg + (3 * G + 1))
                v.tensor_tensor(R_[:, js, :], bank(4, G * D).rearrange("p (i f) -> p i f", i=G),
                                rows[:, 4, :].unsqueeze(1).to_broadcast([P, G, D]), ALU.add).then_inc(prod_read, 1)
                dve.wait_ge(prod_read, gg + (3 * G + 1))
            dve.sem_inc(rows_ready, 1)
            leave(dve, 5)

            v.memset(zeros, 0.0).then_inc(zeros_ready, 1)
            v.memset(ea3w, 0.0).then_inc(zeros_ready, 1)
            with dve.Fori(0, T) as t:
                for u in range(U):
                    for i in range(G):
                        c = t * (U * G) + (G * u + i)
                        onehots(c + NC, c, G * u + i)
                    dve.wait_ge(gathered[u], t * (16 * G) + 16 * G)
                    dve.wait_ge(ew_ready, t * U + (u + 1))
                    m = msg[0:P, G * u:G * u + G, :]
                    v.tensor_tensor(m, m, bank(4 + u, G * D).rearrange("p (i f) -> p i f", i=G), ALU.add).then_inc(premsg_ready, 1)
            leave(dve, 6)

            hn = psum[0:P, 0:4, :].rearrange("p b k -> p (b k)")[:, 0:BLK].rearrange("p (j f) -> p j f", j=NB)
            with dve.Fori(0, G) as gg:
                chain.enter(gg, 3)
                js = ds(gg * G, G)
                link(v.tensor_copy(cat[:, :, 0:D], H_[:, js, :]))
                v.tensor_copy(cat[:, :, D:2 * D], hn[:, js, :]).then_inc(cat_ready, 1)
                dve.wait_ge(prod_ready, gg + (4 * G + 1))
                link(v.tensor_scalar(R_[:, js, :], bank(6, G * D).rearrange("p (i f) -> p i f", i=G), 0.0, None, ALU.max))
                link(v.tensor_tensor(X_[:, js, :], X_[:, js, :], R_[:, js, :], ALU.add))
                chain.leave(G)
            leave(dve, 7)

            layernorm(X_)
            dve.wait_ge(outdeg_ready, 1)
            link(v.tensor_reduce(norm_out, outdeg4[:, :, :], X, ALU.add))
            link(v.tensor_scalar(norm_in, indeg1, -1.0, 1.0, ALU.add, ALU.max))
            std(v.tensor_scalar(norm_out, norm_out, 1.0, None, ALU.max))
            link(v.reciprocal(norm_in, norm_in))
            link(v.reciprocal(norm_out, norm_out))
            link(v.tensor_tensor(H_, H_, over_f(norm_out), ALU.mult))
            split()
            take(2, lambda j: link(v.scalar_tensor_tensor(out=X_[:, ds(j, 1), :], in0=ysum[:, :].unsqueeze(1),
                                                          scalar=norm_in[:, ds(j, 1)], in1=X_[:, ds(j, 1), :],
                                                          op0=ALU.mult, op1=ALU.add)))
            leave(dve, 8)

            layernorm(X_)
            split()
            take(2, lambda j: link(v.tensor_tensor(X_[:, ds(j, 1), :], X_[:, ds(j, 1), :], ysum[:, :].unsqueeze(1), ALU.add)))
            leave(dve, 9)


_INS = ["x", "src", "dst", "edge_attr_16", "edge_attr_3",
        "L0_gnn_W0", "L0_gnn_b0", "L0_gnn_W1", "L0_gnn_b1", "L0_gnn_W2", "L0_gnn_b2",
        "L0_gnn_g0", "L0_gnn_be0", "L0_gnn_g1", "L0_gnn_be1", "L1_gnn_W1", "L1_gnn_b1", "L1_gnn_W2"]


def kernel(**inputs):
    import numpy as _np
    import concourse.bacc as _bacc
    from concourse import mybir as _mybir
    from concourse.bass_utils import run_bass_kernel_spmd as _run

    nc = _bacc.Bacc("TRN2", target_bir_lowering=False, num_devices=1)
    arrays, args = {}, []
    for name in _INS:
        a = _np.ascontiguousarray(inputs[name])
        arrays[f"in_{name}_dram"] = a
        args.append(nc.dram_tensor(f"in_{name}_dram", a.shape, _mybir.dt.from_np(a.dtype), kind="ExternalInput").ap())
    args.append(nc.dram_tensor("out_0_dram", (N, D), F32, kind="ExternalOutput").ap())
    build(nc, *args)
    r = _run(nc, [arrays], core_ids=[0])
    return r.results[0]["out_0_dram"]
```

```python
from contextlib import ExitStack

import concourse.bass as bass
from concourse import mybir

F32 = mybir.dt.float32
BF16 = mybir.dt.bfloat16
F16 = mybir.dt.float16
I32 = mybir.dt.int32
I16 = mybir.dt.int16
ALU = mybir.AluOpType
ACT = mybir.ActivationFunctionType
X = mybir.AxisListType.X
ds = bass.ds

N, E, D = 3125, 103125, 64
P = 125
NB = N // P
NC = E // P
EF = 16
EX = EF + 1
CT, CP = 15, 55
HALF = 9
W = 20
WP = -(-N // (2 * W))
NW = 2 * WP
WK = W * NB
DP = NW * W
G, U = 5, 3
T = NC // (G * U)
K = 7
KQ = NC + K
EPS = 1e-5
LANES = ((0, 112), (112, P))
SPLIT = ((0, 0, HALF), (1, HALF, CT))


class Chain:

    def __init__(self, engine, sem):
        self.engine, self.sem, self.base, self.t, self.per, self.steps = engine, sem, 0, None, 0, 0

    def link(self, instruction):
        instruction.then_inc(self.sem, 1)
        self.steps += 1
        done = self.base + self.steps
        self.engine.wait_ge(self.sem, done if self.t is None else self.t * self.per + done)

    def enter(self, t, per):
        self.base, self.t, self.per, self.steps = self.base + self.steps, t, per, 0

    def leave(self, trips):
        assert self.steps == self.per, (self.steps, self.per)
        self.base, self.t, self.steps = self.base + trips * self.per, None, 0


def build(nc, x, src, dst, ea16, ea3, w0, b0, w1, b1, w2, b2, g0, be0, g1, be1, mw1, mb1, mw2, out):
    with ExitStack() as ctx:
        ctx.enter_context(nc.allow_non_contiguous_dma(reason="bias columns"))

        def sb(name, shape, dt):
            return ctx.enter_context(nc.sbuf_tensor(name, shape, dt))

        def sem(name):
            return ctx.enter_context(nc.semaphore(name))

        AT = sb("AT", [P, NB * DP], BF16)
        at3 = AT[:, :].rearrange("p (b d) -> p b d", b=NB)
        dstf = sb("dstf", [P, NC], F32)
        srci = sb("srci", [128, NC + G], I32)
        ident = sb("ident", [128, 128], F32)
        ones = sb("ones", [128, P], F32)
        tabs = sb("tabs", [P, P], F16)
        nbj = sb("nbj", [P, NB], F32)
        Wcat = sb("Wcat", [128, 3, D], F32)
        Wex = sb("Wex", [EX, 3, D], F32)
        W1a = sb("W1a", [D, D], F32)
        W2s = sb("W2s", [128, D], F32)
        rows = sb("rows", [P, 5, D], F32)
        schedj = sb("schedj", [1, NC // G, 2], I16)
        stat = sb("stat", [P, 4, D], F32)
        node = sb("node", [P, 6, NB], F32)
        ysum = sb("ysum", [P, D], F32)
        outdeg4 = sb("outdeg4", [P, NB, 4], F32)
        ARENA = 9605
        arena = sb("arena", [128, ARENA], F32)
        psum = ctx.enter_context(nc.psum_tensor("psum", [128, 8, 512], F32))
        mean_n, var_n, indeg1, norm_in, norm_out, tmp_n = (node[:, i, :] for i in range(6))
        fsum, fsq, scale_f, tmp_f = (stat[:, i, :] for i in range(4))

        def area(at, size, p=P):
            assert at + size <= ARENA, (at, size)
            return arena[0:p, at:at + size]

        BLK = NB * D
        X_ = area(0, BLK).rearrange("p (j f) -> p j f", j=NB)
        H_ = area(BLK, BLK).rearrange("p (j f) -> p j f", j=NB)
        R_ = area(2 * BLK, BLK).rearrange("p (j f) -> p j f", j=NB)
        zs = area(3 * BLK, 3 * BLK // 2).bitcast(BF16).rearrange("p (j k f) -> p j k f", j=NB, k=3)
        SQ = area(3 * BLK, BLK).rearrange("p (j f) -> p j f", j=NB)
        cat_at = 3 * BLK + 3 * BLK // 2
        cat = area(cat_at, G * 128).rearrange("p (i f) -> p i f", i=G)
        rz = area(cat_at, G * D).rearrange("p (i f) -> p i f", i=G)
        catT = area(cat_at + 725, G * P, 128).rearrange("p (i f) -> p i f", i=G)
        junk = area(cat_at + 725, G * P).bitcast(BF16)
        eacT = area(cat_at + 1350, G * P, EX).rearrange("p (i f) -> p i f", i=G)
        kq = area(0, 3 * KQ).rearrange("p (c k) -> p c k", k=3)
        tabk = area(2496, WK // 2).bitcast(F16)
        nbw = area(2746, 3 * NW).rearrange("p (w k) -> p w k", k=3)
        krel = area(3220, 3 * K).rearrange("p (c k) -> p c k", k=3)
        schedw = area(3242, NW, 1).bitcast(I16)
        zeros = area(3400, 256).bitcast(BF16)
        ohs = area(3656, K * 64).bitcast(BF16).rearrange("p (i d) -> p i d", i=K)
        ohk = area(4104, K * WK // 2).bitcast(BF16).rearrange("p (i d) -> p i d", i=K)
        ohd = area(5854, K * W).rearrange("p (i d) -> p i d", i=K)
        eaw = area(5994, 2 * K * EX).rearrange("p (h i f) -> p h i f", h=2, f=EX)
        eaS = area(6240, DP, EX)
        drel = area(3200, U * G).rearrange("p (i d) -> p i d", i=U)
        zeros_m = area(3220, 256).bitcast(BF16)
        oh = area(3810, U * G * P).rearrange("p (i d) -> p i d", i=U * G)
        msg = area(5810, U * G * D, 128).rearrange("p (i f) -> p i f", i=U * G)
        ea3s = area(6770, U * 3 * P, G).rearrange("p (i e k) -> p i e k", i=U, e=P)
        ea3w = area(7895, 3 * G * D, G).rearrange("p (k i f) -> p k i f", k=3, i=G)
        ring = area(8855, U * G, 128).bitcast(I32)
        zidx = area(8870, G, 128).bitcast(I32)
        atf = AT[:, :].bitcast(F32)

        def early(at, size, p=P):
            return atf[0:p, at:at + size]

        dnat = early(0, CT * P, CP).bitcast(I32).rearrange("p (t e) -> p t e", t=CT)
        snat = early(1875, CT * P, CP).bitcast(I32).rearrange("p (t e) -> p t e", t=CT)
        dnf = early(3750, CT * P, CP).rearrange("p (t e) -> p t e", t=CT)
        diag = early(5625, 2 * NC, CP).rearrange("p (k t r) -> p k t r", k=2, t=CT)
        m1, m2, m3 = early(7275, NC, WP), early(8100, NC, WP), early(8925, NC, WP)
        up = early(9750, NC, WP)
        down = early(10575, NC, WP)
        qf = early(11400, NC)
        qi = early(12225, NC).bitcast(I32)
        rf = early(13050, NC)
        eaT = early(14000, KQ * EX).rearrange("p (c f) -> p c f", c=KQ)
        eas = early(28150, U * P * EF, CP).rearrange("p (i e f) -> p i e f", i=U, f=EF)
        cmpj = early(38440, CT * (NB - 1), CP).rearrange("p (t j) -> p t j", t=CT)
        jtab = early(34500, NB - 1, CP)
        wlo, whi = early(34530, 2, WP), early(34532, 2, WP)
        dmm = early(34540, 2 * CT, CP).rearrange("p (k t) -> p k t", k=2)
        jmm = early(34570, 2 * CT, CP).rearrange("p (k t) -> p k t", k=2)
        wm = early(34600, 4, WP)
        srcf = early(34700, NC)
        snf = early(36000, CT * P, CP).rearrange("p (t e) -> p t e", t=CT)
        wraw = early(38000, 3 * 145, D).rearrange("p (l f) -> p l f", l=3)

        src_v = src.rearrange("(t r e) -> r t e", t=CT, r=CP)
        dst_v = dst.rearrange("(t r e) -> r t e", t=CT, r=CP)
        ea16_v = ea16.rearrange("(c e) f -> c e f", e=P)
        ea3_v = ea3.rearrange("(c e) k -> c e k", e=P)
        x_v = x.rearrange("(j q) f -> q j f", q=P)
        out_v = out.rearrange("(j q) f -> q j f", q=P)
        eaD = nc.dram_tensor("ea_by_place", (P, KQ, EX), F32).ap()
        eaSD = nc.dram_tensor("ea_sums", (EX, N), F32).ap()
        msgsrc = nc.dram_tensor("msgsrc", (N, D), F32).ap()
        msgsrc_v = msgsrc.rearrange("(j q) f -> q j f", q=P)

        phase_left = sem("phase_left")
        idx_in, w_in, x_in, x_again, ea3w_in = (sem(n) for n in ("idx_in", "w_in", "x_in", "x_again", "ea3w_in"))
        ea_in = [sem(f"ea_in{i}") for i in range(U)]
        ea3_in = [sem(f"ea3_in{i}") for i in range(U)]
        gathered = [sem(f"gathered{i}") for i in range(U)]
        drel_ready, krel_ready = sem("drel_ready"), sem("krel_ready")
        tables, dve_step, act_step = sem("tables"), sem("dve_step"), sem("act_step")
        idx_f32, idx_T, idx_copied = sem("idx_f32"), sem("idx_T"), sem("idx_copied")
        diag_ready, diag_sum, sums_read = sem("diag_ready"), sem("diag_sum"), sem("sums_read")
        win_ready, win_T, w_T = sem("win_ready"), sem("win_T"), sem("w_T")
        ea_T, ea_half_act, ea_half_dve = sem("ea_T"), sem("ea_half_act"), sem("ea_half_dve")
        pads_ready, ea_stored = sem("pads_ready"), sem("ea_stored")
        eaw_in = [sem(f"eaw_in{h}") for h in range(2)]
        ohd_ready, eaw_used, eaS_ready, eaS_stored = sem("ohd_ready"), sem("eaw_used"), sem("eaS_ready"), sem("eaS_stored")
        indeg_ready, eacT_in = sem("indeg_ready"), sem("eacT_in")
        oh_ready, oh_used = sem("oh_ready"), sem("oh_used")
        group_used, zeros_ready = sem("group_used"), sem("zeros_ready")
        pair_ready, pair_used, window_done, window_kept = sem("pair_ready"), sem("pair_used"), sem("window_done"), sem("window_kept")
        cat_ready, cat_T, catT_ready = sem("cat_ready"), sem("cat_T"), sem("catT_ready")
        prod_ready, prod_read, z1_ready = sem("prod_ready"), sem("prod_read"), sem("z1_ready")
        y_ready, y_free, zs_ready = sem("y_ready"), sem("y_free"), sem("zs_ready")
        fsum_ready, fsum_total, var_ready, std_ready = sem("fsum_ready"), sem("fsum_total"), sem("var_ready"), sem("std_ready")
        outdeg_ready, rows_ready, rows_out, out_done = sem("outdeg_ready"), sem("rows_ready"), sem("rows_out"), sem("out_done")
        ring_ready, ew_ready, premsg_ready, msg_ready = sem("ring_ready"), sem("ew_ready"), sem("premsg_ready"), sem("msg_ready")

        block = ctx.enter_context(nc.Block())
        NTAB = 14
        NWIN = 12 + 2 + 5

        def leave(eng, n):
            eng.drain().then_inc(phase_left, 1)
            eng.wait_ge(phase_left, 5 * n)

        def load_range(eng, pair, at, most):
            eng.load(list(pair), at)
            return eng.snap(pair[0], min_val=0, max_val=most - 1), eng.snap(pair[1], min_val=1, max_val=most)

        def bank(b, cols, p=P):
            return psum[0:p, b, 0:cols]

        @block.sync
        def _(sp):
            sp.dma_start(dnat, dst_v).then_inc(idx_in, 16)
            sp.dma_start(snat, src_v).then_inc(idx_in, 16)
            for l, (w, b) in enumerate(((w0, b0), (w1, b1), (w2, b2))):
                sp.dma_start(wraw[:, l, 0:D], w[:, D:2 * D]).then_inc(w_in, 16)
                sp.dma_start(wraw[:, l, D:2 * D], w[:, 0:D]).then_inc(w_in, 16)
                sp.dma_start(wraw[:, l, 2 * D:2 * D + EF], w[:, 2 * D:2 * D + EF]).then_inc(w_in, 16)
                sp.dma_start(wraw[:, l, 2 * D + EF:2 * D + EX], b.rearrange("(f a) -> f a", a=1)).then_inc(w_in, 16)
            sp.dma_start(W1a[:, :], mw1[0:D, :]).then_inc(w_in, 16)
            sp.dma_start(W2s[:, :], mw2[:, :]).then_inc(w_in, 16)
            for k, r in enumerate((g0, be0, g1, be1, mb1)):
                sp.dma_start(rows[:, k, :], r.rearrange("(a f) -> a f", a=1).to_broadcast([P, D])).then_inc(w_in, 16)
            def load_tile(n, u):
                sp.dma_start(eas[:, u, :, :], ea16_v[ds(n * CP, CP)]).then_inc(ea_in[u], 16)

            def store_tile(n):
                for a, b in LANES:
                    sp.dma_start(eaD[a:b, ds(n * CP, CP), :], eaT[a:b, ds(n * CP, CP), :]).then_inc(ea_stored, 16)

            for u in range(U):
                load_tile(u, u)
            sp.wait_ge(pads_ready, 2)
            for a, b in LANES:
                sp.dma_start(eaD[a:b, NC:KQ, :], eaT[a:b, NC:KQ, :]).then_inc(ea_stored, 16)
            with sp.Fori(0, CT // U - 1) as t:
                for u in range(U):
                    sp.wait_ge(ea_half_act, t * U + (u + 1))
                    sp.wait_ge(ea_half_dve, t * U + (u + 1))
                    load_tile(t * U + (u + U), u)
                    store_tile(t * U + u)
            for n in range(CT - U, CT):
                sp.wait_ge(ea_half_act, n + 1)
                sp.wait_ge(ea_half_dve, n + 1)
                store_tile(n)
            sp.wait_ge(ea_stored, (CT + 1) * 16 * len(LANES))
            leave(sp, 1)
            steps = ctx.enter_context(sp.register("steps_sp"))
            need = ctx.enter_context(sp.register("need_sp"))
            pair = [ctx.enter_context(sp.register(f"range_sp{i}")) for i in range(2)]
            sp.reg_mov(steps, 0)
            with sp.Fori(0, NW // 2) as t:
                for h in range(2):
                    start, end = load_range(sp, pair, schedw[0:1, ds((t * 2 + h) * 2, 2)], NC)
                    sp.reg_add(need, steps, 1)
                    with sp.Fori(start, end, K) as c:
                        sp.reg_add(steps, steps, 1)
                        sp.wait_ge(eaw_used, sp.snap(need, min_val=1, max_val=NC * NW))
                        sp.reg_add(need, steps, 2)
                        for a, b in LANES:
                            sp.dma_start(eaw[a:b, h, :, :], eaD[a:b, ds(c, K), :]).then_inc(eaw_in[h], 16)
            sp.wait_ge(eaS_ready, 1)
            sp.dma_start(eaSD, eaS[:, 0:N]).then_inc(eaS_stored, 16)
            sp.wait_ge(eaS_stored, 16)
            leave(sp, 2)
            for a, b in LANES:
                sp.dma_start(R_[a:b], x_v[a:b]).then_inc(x_in, 16)
            for a, b in LANES:
                sp.dma_start(X_[a:b], x_v[a:b]).then_inc(x_again, 16)
            for l in range(3):
                if l == 0:
                    sp.dma_start(eacT, eaSD[:, 0:G * P].rearrange("p (i e) -> p i e", i=G)).then_inc(eacT_in, 16)
                with sp.Fori(0 if l else 1, G) as gg:
                    sp.wait_ge(prod_ready, gg + G * l)
                    sp.dma_start(eacT, eaSD[:, ds(gg * G * P, G * P)].rearrange("p (i e) -> p i e", i=G)).then_inc(eacT_in, 16)
            leave(sp, 3)
            sp.wait_ge(rows_ready, 1)
            for a, b in LANES:
                sp.dma_start(msgsrc_v[a:b], R_[a:b]).then_inc(rows_out, 16)
            sp.wait_ge(rows_out, 16 * len(LANES))
            leave(sp, 4)
            sp.wait_ge(zeros_ready, 2)
            for i in range(G):
                sp.dma_start(ea3w[i:i + 1, :, i, :], mw1[D:D + 3, :].rearrange("(a k) f -> a k f", a=1)).then_inc(ea3w_in, 16)
            with sp.Fori(0, T) as t:
                for u in range(U):
                    sp.wait_ge(group_used, t * U + (u + 1))
                    sp.dma_start(ea3s[:, u, :, :], ea3_v[ds((t * U + u) * G, G)]).then_inc(ea3_in[u], 16)
            for n in range(5, 9):
                leave(sp, n)
            for a, b in LANES:
                sp.dma_start(out_v[a:b], X_[a:b]).then_inc(out_done, 16)
            sp.wait_ge(out_done, 16 * len(LANES))

        @block.gpsimd
        def _(pool):
            g = nc.gpsimd
            loose = dict(allow_small_or_imprecise_dtypes=True)
            g.memset(ident[:, :], 0.0).then_inc(tables, 1)
            g.memset(ones[:, :], 1.0).then_inc(tables, 1)
            g.iota(tabs[:, :], pattern=[[1, P]], base=0, channel_multiplier=0, **loose).then_inc(tables, 1)
            g.iota(nbj[:, :], pattern=[[-P, NB]], base=0, channel_multiplier=0, **loose).then_inc(tables, 1)
            g.iota(tabk, pattern=[[1, NB], [NB, W]], base=0, channel_multiplier=0, **loose).then_inc(tables, 1)
            g.iota(nbw[:, :, 0], pattern=[[-WK, NW]], base=0, channel_multiplier=0, **loose).then_inc(tables, 1)
            g.iota(up, pattern=[[1, NC]], base=1, channel_multiplier=0, **loose).then_inc(tables, 1)
            g.iota(down, pattern=[[-1, NC]], base=NC, channel_multiplier=0, **loose).then_inc(tables, 1)
            g.iota(jtab, pattern=[[P, NB - 1]], base=P, channel_multiplier=0, **loose).then_inc(tables, 1)
            g.iota(wlo, pattern=[[WP * W, 2]], base=0, channel_multiplier=W, **loose).then_inc(tables, 1)
            g.iota(whi, pattern=[[WP * W, 2]], base=W - 1, channel_multiplier=W, **loose).then_inc(tables, 1)
            g.memset(srci[:, :], 0).then_inc(tables, 1)
            g.memset(zeros, 0.0).then_inc(tables, 1)
            pool.wait_ge(tables, 1)
            g.affine_select(out=ident[:, :], in_=ident[:, :], compare_op=ALU.not_equal, fill=1.0, base=0,
                            pattern=[[-1, 128]], channel_multiplier=1).then_inc(tables, 1)
            g.memset(nbw[:, :, 1], 0.0)
            g.iota(nbw[:, :, 2], pattern=[[-W, NW]], base=0, channel_multiplier=0, **loose)
            g.memset(kq[:, NC:KQ, :], -1.0)
            g.memset(eaT[:, :, EF:EX], 1.0).then_inc(pads_ready, 1)
            g.memset(eaT[:, NC:KQ, 0:EF], 0.0).then_inc(pads_ready, 1)
            for n in range(1, 5):
                leave(pool, n)
            g.memset(zidx, 0).then_inc(ring_ready, 1)
            pool.sem_inc(premsg_ready, U - 1)
            pool.wait_ge(ring_ready, 1)
            g.tensor_tensor(ring[:, 0:G], srci[:, 0:G], zidx, ALU.add).then_inc(ring_ready, 1)
            with pool.Fori(0, T) as t:
                for u in range(U):
                    v = (u + 1) % U
                    pool.wait_ge(premsg_ready, t * U + (u + 1))
                    pool.wait_ge(group_used, t * U + (u + 1))
                    pool.wait_ge(ring_ready, t * U + (u + 2))
                    g.tensor_tensor(ring[:, G * v:G * v + G], srci[:, ds((t * U + (u + 1)) * G, G)], zidx,
                                    ALU.add).then_inc(ring_ready, 1)
                    for i in range(G * u, G * u + G):
                        g.indirect_dma_start(msg[:, i, :], None, msgsrc,
                                             bass.IndirectOffsetOnAxis(ring[:, i:i + 1], 0)).then_inc(gathered[u], 16)
            for n in range(5, 9):
                leave(pool, n)

        @block.scalar
        def _(act):
            a = nc.scalar
            chain = Chain(act, act_step)
            with act.Fori(0, CT // U) as t:
                for u in range(U):
                    act.wait_ge(ea_T, t * U + (u + 1))
                    a.copy(eaT[:, ds((t * U + u) * CP, CP), 0:EF // 2].rearrange("p c f -> p f c"),
                           bank(2 * u, 8 * CP).rearrange("p (f c) -> p f c", f=8)).then_inc(ea_half_act, 1)
            leave(act, 1)
            act.sem_inc(window_kept, 2)
            with act.Fori(0, NW // 2) as t:
                for h in range(2):
                    act.wait_ge(window_done, t * 2 + (h + 1))
                    a.copy(at3[:, :, ds((t * 2 + h) * W, W)], bank(1 + h, WK).rearrange("p (b d) -> p b d", d=W))
                    a.copy(eaS[:, ds((t * 2 + h) * W, W)], bank(3 + h, W, EX)).then_inc(window_kept, 1)
            leave(act, 2)

            def turn(n, nrow, first):
                act.wait_ge(cat_T, n)
                chain.link(a.copy(catT[0:nrow, 0:4, :], bank(first, 4 * P, nrow).rearrange("p (i e) -> p i e", i=4)))
                a.copy(catT[0:nrow, 4, :], bank(first + 1, P, nrow)).then_inc(catT_ready, 1)

            roots = [0]

            def root():
                act.wait_ge(var_ready, roots[0] + 1)
                roots[0] += 1
                return roots[0]

            def node_root():
                root()
                a.activation(tmp_n, var_n, ACT.Sqrt).then_inc(std_ready, 1)

            node_root()
            for l in range(3):
                with act.Fori(0, G) as gg:
                    chain.enter(gg, 1)
                    turn(gg + (G * l + 1), 128, 0)
                    chain.leave(G)
                    act.wait_ge(prod_ready, gg + (G * l + 1))
                    a.copy(zs[:, ds(gg * G, G), 0, :], bank(4, G * D).rearrange("p (i f) -> p i f", i=G)).then_inc(z1_ready, 1)
                if l == 0:
                    with act.Fori(0, NB) as b:
                        chain.enter(b, 4)
                        for k in range(4):
                            w4 = DP // 4
                            chain.link(a.activation(junk[:, 0:w4], at3[:, ds(b, 1), k * w4:(k + 1) * w4].rearrange("p a d -> p (a d)"),
                                                    ACT.Copy, accum_out=outdeg4[:, ds(b, 1), k:k + 1].rearrange("p a k -> p (a k)")))
                        chain.leave(NB)
                    act.sem_inc(outdeg_ready, 1)
                if l < 2:
                    root()
                    a.activation(tmp_f, fsq, ACT.Sqrt).then_inc(std_ready, 1)
            leave(act, 3)
            node_root()
            with act.Fori(0, G) as gg:
                chain.enter(gg, 1)
                turn(gg + (3 * G + 1), 128, 0)
                chain.leave(G)
            leave(act, 4)
            with act.Fori(0, T) as t:
                for u in range(U):
                    act.wait_ge(premsg_ready, t * U + (u + U))
                    m = msg[0:P, G * u:G * u + G, :]
                    a.activation(m, m, ACT.Relu).then_inc(msg_ready, 1)
            leave(act, 5)
            with act.Fori(0, G) as gg:
                chain.enter(gg, 1)
                turn(gg + (4 * G + 1), 128, 4)
                chain.leave(G)
            leave(act, 6)
            node_root()
            root()
            chain.link(a.activation(norm_in, norm_in, ACT.Sqrt))
            a.activation(norm_out, norm_out, ACT.Sqrt).then_inc(std_ready, 1)
            leave(act, 7)
            node_root()
            leave(act, 8)

        @block.tensor
        def _(pe):
            mm, tp = nc.tensor.matmul, nc.tensor.transpose
            pe.wait_ge(tables, NTAB)
            for k, nat in enumerate((dnf, snf)):
                pe.wait_ge(idx_f32, k + 1)
                for b, lo, hi in SPLIT:
                    for t in range(lo, hi):
                        last = tp(psum[0:P, 2 * k + b, (t - lo) * CP:(t - lo + 1) * CP], nat[:, t, :], ident[0:CP, 0:CP])
                last.then_inc(idx_T, 1)
            pe.wait_ge(diag_ready, 1)
            for k in range(2):
                for b, lo, hi in SPLIT:
                    last = mm(bank(4 + 2 * k + b, (hi - lo) * CP, WP), ones[0:CP, 0:WP],
                              diag[:, k, lo:hi, :].rearrange("p t r -> p (t r)"), start=True, stop=True)
            last.then_inc(diag_sum, 1)
            pe.wait_ge(idx_copied, 4)
            pe.wait_ge(diag_ready, 2)
            for k in range(2):
                for b, lo, hi in SPLIT:
                    last = mm(bank(2 * k + b, (hi - lo) * CP, 1), ones[0:CP, 0:1],
                              diag[:, k, lo:hi, :].rearrange("p t r -> p (t r)"), start=True, stop=True)
            last.then_inc(diag_sum, 1)
            pe.wait_ge(win_ready, 1)
            for k in range(4):
                last = mm(psum[0:1, 4, k * WP:(k + 1) * WP], wm[:, k:k + 1], ident[0:WP, 0:WP], start=True, stop=True)
            last.then_inc(win_T, 1)
            pe.wait_ge(w_in, 16 * NWIN)
            for l in range(3):
                tp(psum[:, 7, l * D:(l + 1) * D], wraw[:, l, 0:128], ident[0:D, 0:D])
                last = tp(psum[0:EX, 6, l * D:(l + 1) * D], wraw[:, l, 128:128 + EX], ident[0:D, 0:D])
            last.then_inc(w_T, 1)
            pe.wait_ge(sums_read, 3)
            with pe.Fori(0, CT // U) as t:
                for u in range(U):
                    pe.wait_ge(ea_in[u], t * 16 + 16)
                    mm(psum[0:P, 7, 0:1], ones[0:CP, 0:P], ones[0:CP, 0:1], start=True, stop=True)
                    for f in range(EF):
                        last = tp(psum[0:P, 2 * u + f // 8, (f % 8) * CP:(f % 8 + 1) * CP], eas[:, u, :, f], ident[0:CP, 0:CP])
                    last.then_inc(ea_T, 1)
            leave(pe, 1)

            pe.sem_inc(oh_used, 2)
            units = ctx.enter_context(pe.register("units_pe"))
            pair = [ctx.enter_context(pe.register(f"range_pe{i}")) for i in range(2)]
            pe.reg_mov(units, 0)

            def scatter_group(grp, u, place, payload):
                lo, end = load_range(pe, pair, schedj[0:1, ds(grp, 1), :].rearrange("p a b -> p (a b)"), NB)
                with pe.Fori(lo, end) as j:
                    pe.reg_add(units, units, 1)
                    pe.wait_ge(oh_ready, pe.snap(units, min_val=1, max_val=2 * NC * NB))
                    for i in range(G):
                        last = mm(place(j), oh[:, G * u + i, :], payload(i), start=False, stop=False, skip_group_check=True)
                    last.then_inc(oh_used, 1)

            def zero(banks, z):
                for b in banks:
                    last = mm(bank(b, 512), z[:, 0:P], z[:, 0:512], start=True, stop=True)
                return last

            pe.sem_inc(pair_used, K)
            pe.sem_inc(eaw_used, 2)
            pairs = ctx.enter_context(pe.register("pairs_pe"))
            steps = ctx.enter_context(pe.register("steps_pe"))
            landed = [ctx.enter_context(pe.register(f"landed_pe{h}")) for h in range(2)]
            for reg in [pairs, steps] + landed:
                pe.reg_mov(reg, 0)
            with pe.Fori(0, NW // 2) as t:
                for h in range(2):
                    start, end = load_range(pe, pair, schedw[0:1, ds((t * 2 + h) * 2, 2)], NC)
                    pe.wait_ge(window_kept, t * 2 + (h + 1))
                    mm(bank(1 + h, WK), zeros[:, 0:P], zeros[:, 0:WK], start=True, stop=True)
                    mm(bank(3 + h, W, EX), zeros[:, 0:EX], zeros[:, 0:W], start=True, stop=True)
                    with pe.Fori(start, end, K):
                        done = pe.snap(pairs, min_val=0, max_val=NC * NW)
                        for k in range(K):
                            pe.wait_ge(pair_ready, done + (k + 1))
                            mm(bank(1 + h, WK), ohs[:, k, 0:P], ohk[:, k, :], start=False, stop=False,
                               skip_group_check=True).then_inc(pair_used, 1)
                        pe.reg_add(pairs, pairs, K)
                        pe.reg_add(steps, steps, 1)
                        pe.reg_add(landed[h], landed[h], 16 * len(LANES))
                        step, in_place = pe.snap(steps, min_val=1, max_val=NC * NW), pe.snap(landed[h], min_val=1, max_val=32 * NC * NW)
                        pe.wait_ge(ohd_ready, step + 1)
                        pe.wait_ge(eaw_in[h], in_place)
                        for k in range(K):
                            last = mm(bank(3 + h, W, EX), eaw[:, h, k, :], ohd[:, k, :], start=False, stop=False,
                                      skip_group_check=True)
                        last.then_inc(eaw_used, 1)
                    mm(bank(1 + h, 1), zeros[:, 0:P], zeros[:, 0:1], start=False, stop=True,
                       skip_group_check=True).then_inc(window_done, 1)
            pe.wait_ge(eaS_ready, 1)
            for j in range(NB):
                last = mm(psum[0:P, 5, j:j + 1], eaS[:, j * P:(j + 1) * P], ident[0:EX, EF:EX], start=True, stop=True)
            last.then_inc(indeg_ready, 1)
            leave(pe, 2)

            def turn(n, nrow, first):
                pe.wait_ge(cat_ready, n)
                for i in range(G):
                    last = tp(psum[0:nrow, first + i // 4, (i % 4) * P:(i % 4 + 1) * P], cat[:, i, 0:nrow], ident[0:P, 0:P])
                last.then_inc(cat_T, 1)
                pe.wait_ge(catT_ready, n)

            applied = [0]

            def apply():
                base = NB * applied[0]
                applied[0] += 1
                pe.wait_ge(zs_ready, applied[0])
                with pe.Fori(0, G) as gg:
                    for u in range(G):
                        pe.wait_ge(y_free, gg * G + (base + u + 1))
                        for b in range(NB):
                            last = mm(bank(u, 3 * D), at3[:, b, ds((gg * G + u) * P, P)],
                                      zs[:, b, :, :].rearrange("p k f -> p (k f)"), start=(b == 0), stop=(b == NB - 1))
                        last.then_inc(y_ready, 1)

            totals = [0]

            def total():
                totals[0] += 1
                pe.wait_ge(fsum_ready, totals[0])
                mm(bank(6, D), ones[0:P, 0:P], fsum, start=True, stop=True).then_inc(fsum_total, 1)

            pe.sem_inc(y_free, G)
            for l in range(3):
                with pe.Fori(0, G) as gg:
                    turn(gg + (G * l + 1), 128, 0)
                    for i in range(G):
                        mm(psum[0:P, 4, i * D:(i + 1) * D], catT[0:D, i, :], Wcat[0:D, l, :], start=True, stop=True)
                    for i in range(G):
                        o = psum[0:P, 5, i * D:(i + 1) * D]
                        mm(o, catT[:, i, :], Wcat[:, l, :], start=True, stop=False)
                        if i == 0:
                            pe.wait_ge(eacT_in, gg * 16 + (16 * G * l + 16))
                        last = mm(o, eacT[:, i, :], Wex[:, l, :], start=False, stop=True)
                    last.then_inc(prod_ready, 1)
                apply()
                if l < 2:
                    total()
                    total()
            leave(pe, 3)
            with pe.Fori(0, G) as gg:
                turn(gg + (3 * G + 1), 128, 0)
                for i in range(G):
                    last = mm(psum[0:P, 4, i * D:(i + 1) * D], catT[0:D, i, :], W1a[:, :], start=True, stop=True)
                last.then_inc(prod_ready, 1)
            leave(pe, 4)
            pe.wait_ge(zeros_ready, 2)
            zero(range(4), zeros_m)
            pe.sem_inc(group_used, U)
            pe.wait_ge(ea3w_in, 16 * G)

            def edges_part(t, u):
                pe.wait_ge(ea3_in[u], t * 16 + 16)
                for k in range(3):
                    last = mm(bank(4 + u, G * D), ea3s[:, u, :, k], ea3w[:, k, :, :].rearrange("p i f -> p (i f)"),
                              start=(k == 0), stop=(k == 2))
                last.then_inc(ew_ready, 1)

            def sum_messages(t, u):
                pe.wait_ge(msg_ready, t * U + (u + 1))
                scatter_group(t * U + u, u, lambda j: psum[0:P, 0:4, :].rearrange("p b k -> p (b k)")[:, ds(j * D, D)],
                              lambda i: msg[0:P, G * u + i, :])
                mm(psum[0:P, 7, 0:1], zeros_m[:, 0:P], zeros_m[:, 0:1], start=True, stop=True).then_inc(group_used, 1)

            edges_part(0, 0)
            with pe.Fori(0, T - 1) as t:
                for u in range(U):
                    edges_part(t + (u + 1) // U, (u + 1) % U)
                    sum_messages(t, u)
            for u in range(U):
                if u + 1 < U:
                    edges_part(T - 1, u + 1)
                sum_messages(T - 1, u)
            leave(pe, 5)
            with pe.Fori(0, G) as gg:
                turn(gg + (4 * G + 1), 128, 4)
                for i in range(G):
                    last = mm(psum[0:P, 6, i * D:(i + 1) * D], catT[:, i, :], W2s[:, :], start=True, stop=True)
                last.then_inc(prod_ready, 1)
            leave(pe, 6)
            apply()
            leave(pe, 7)
            apply()
            leave(pe, 8)

        @block.vector
        def _(dve):
            v = nc.vector
            chain = Chain(dve, dve_step)
            link = chain.link
            dve.wait_ge(idx_in, 32)
            v.tensor_copy(dnf, dnat).then_inc(idx_f32, 1)
            v.tensor_copy(snf, snat).then_inc(idx_f32, 1)
            dve.wait_ge(idx_f32, 1)
            dve.wait_ge(tables, NTAB)
            link(v.tensor_reduce(dmm[:, 0, :], dnf, X, ALU.min))
            link(v.tensor_reduce(dmm[:, 1, :], dnf, X, ALU.max))
            rr = ident[0:CP, 0:CP].unsqueeze(1).to_broadcast([CP, CT, CP])

            def diagonal(vals):
                for k in range(2):
                    link(v.tensor_tensor(diag[:, k, :, :], rr, vals[:, k, :].unsqueeze(2).to_broadcast([CP, CT, CP]), ALU.mult))

            diagonal(dmm)
            dve.sem_inc(diag_ready, 1)
            for k in range(2):
                link(v.tensor_tensor(cmpj, dmm[:, k, :].unsqueeze(2).to_broadcast([CP, CT, NB - 1]),
                                     jtab.unsqueeze(1).to_broadcast([CP, CT, NB - 1]), ALU.is_ge))
                link(v.tensor_reduce(jmm[:, k, :], cmpj, X, ALU.add))
            link(v.tensor_scalar(jmm[:, 1, :], jmm[:, 1, :], 1.0, None, ALU.add))
            for k, col in enumerate((dstf[:, :], srcf)):
                dve.wait_ge(idx_T, k + 1)
                for b, lo, hi in SPLIT:
                    v.tensor_copy(col[:, lo * CP:hi * CP], bank(2 * k + b, (hi - lo) * CP)).then_inc(idx_copied, 1)
            dve.wait_ge(diag_sum, 1)
            diagonal(jmm)
            dve.sem_inc(diag_ready, 1)
            dve.wait_ge(idx_copied, 4)
            v.tensor_copy(srci[0:P, 0:NC], srcf)
            link(v.tensor_scalar(qi, srcf, 1.0 / P, -0.5 + 0.5 / P, ALU.mult, ALU.add))
            link(v.tensor_copy(qf, qi))
            link(v.scalar_tensor_tensor(out=rf, in0=qf, scalar=-float(P), in1=srcf, op0=ALU.mult, op1=ALU.add))
            link(v.scalar_tensor_tensor(out=qf, in0=rf, scalar=float(P), in1=qf, op0=ALU.is_ge, op1=ALU.add))
            link(v.tensor_scalar(rf, rf, 0.0, None, ALU.is_lt))
            link(v.tensor_tensor(qf, qf, rf, ALU.subtract))
            link(v.scalar_tensor_tensor(out=kq[:, 0:NC, 1], in0=qf, scalar=-float(P), in1=srcf, op0=ALU.mult, op1=ALU.add))
            link(v.tensor_copy(kq[:, 0:NC, 2], dstf[:, :]))
            link(v.scalar_tensor_tensor(out=kq[:, 0:NC, 0], in0=dstf[:, :], scalar=float(NB), in1=qf, op0=ALU.mult, op1=ALU.add))
            for h in range(2):
                ws, we = (wm[:, 2 * h + k:2 * h + k + 1] for k in range(2))
                for b, lo, hi in SPLIT:
                    s = slice(lo * CP, hi * CP)
                    link(v.tensor_scalar(m1[:, s], bank(4 + b, (hi - lo) * CP, WP), whi[:, h:h + 1], None, ALU.is_le))
                    link(v.scalar_tensor_tensor(out=m2[:, s], in0=bank(6 + b, (hi - lo) * CP, WP), scalar=wlo[:, h:h + 1],
                                                in1=m1[:, s], op0=ALU.is_ge, op1=ALU.mult))
                link(v.tensor_tensor(m3, m2, up, ALU.mult))
                link(v.tensor_reduce(we, m3, X, ALU.max))
                link(v.tensor_tensor(m3, m2, down, ALU.mult))
                link(v.tensor_reduce(ws, m3, X, ALU.max))
                link(v.tensor_scalar(we, we, 1.0, None, ALU.max))
                link(v.tensor_scalar(ws, ws, -1.0, float(NC), ALU.mult, ALU.add))
                link(v.scalar_tensor_tensor(out=ws, in0=we, scalar=-1.0,
                                            in1=ws, op0=ALU.add, op1=ALU.min))
            dve.sem_inc(win_ready, 1)
            dve.wait_ge(diag_sum, 2)
            for k, op in enumerate((ALU.min, ALU.max)):
                for b, lo, hi in SPLIT:
                    last = v.tensor_reduce(schedj[:, lo * CP // G:hi * CP // G, k:k + 1].rearrange("p c a -> p (c a)"),
                                           bank(2 * k + b, (hi - lo) * CP, 1).rearrange("p (g i) -> p g i", i=G), X, op)
            last.then_inc(sums_read, 1)
            dve.wait_ge(win_T, 1)
            for h in range(2):
                for k in range(2):
                    last = v.tensor_copy(schedw[:, 2 * h * WP:2 * (h + 1) * WP].rearrange("p (w k) -> p w k", k=2)[:, :, k],
                                         psum[0:1, 4, (2 * h + k) * WP:(2 * h + k + 1) * WP])
            last.then_inc(sums_read, 1)
            dve.wait_ge(w_T, 1)
            link(v.tensor_copy(Wcat[:, :, :], psum[:, 7, 0:3 * D].rearrange("p (l f) -> p l f", l=3)))
            link(v.tensor_copy(Wex[:, :, :], psum[0:EX, 6, 0:3 * D].rearrange("p (l f) -> p l f", l=3)))
            dve.sem_inc(sums_read, 1)
            with dve.Fori(0, CT // U) as t:
                for u in range(U):
                    dve.wait_ge(ea_T, t * U + (u + 1))
                    v.tensor_copy(eaT[:, ds((t * U + u) * CP, CP), EF // 2:EF].rearrange("p c f -> p f c"),
                                  bank(2 * u + 1, 8 * CP).rearrange("p (f c) -> p f c", f=8)).then_inc(ea_half_dve, 1)
            leave(dve, 1)

            units = ctx.enter_context(dve.register("units_dve"))
            need = ctx.enter_context(dve.register("need_dve"))
            pair = [ctx.enter_context(dve.register(f"range_dve{i}")) for i in range(2)]
            dve.reg_mov(units, 0)

            def onehots(grp, u):
                lo, end = load_range(dve, pair, schedj[0:1, ds(grp, 1), :].rearrange("p a b -> p (a b)"), NB)
                dve.reg_add(need, units, 1)
                with dve.Fori(lo, end) as j:
                    dve.reg_add(units, units, 1)
                    unit = dve.snap(units, min_val=1, max_val=2 * NC * NB)
                    dve.wait_ge(oh_used, dve.snap(need, min_val=1, max_val=2 * NC * NB))
                    dve.reg_add(need, units, 2)
                    v.tensor_scalar(drel[:, u, :], dstf[:, ds(grp * G, G)], nbj[:, ds(j, 1)], None, ALU.add).then_inc(drel_ready, 1)
                    dve.wait_ge(drel_ready, unit)
                    v.tensor_tensor(oh[:, G * u:G * u + G, :], tabs[:, :].unsqueeze(1).to_broadcast([P, G, P]),
                                    drel[:, u, :].unsqueeze(2).to_broadcast([P, G, P]), ALU.is_equal).then_inc(oh_ready, 1)

            pairs = ctx.enter_context(dve.register("pairs_dve"))
            steps = ctx.enter_context(dve.register("steps_dve"))
            dve.reg_mov(pairs, 0)
            dve.reg_mov(steps, 0)
            dve.sem_inc(ohd_ready, 1)
            with dve.Fori(0, NW) as w:
                start, end = load_range(dve, pair, schedw[0:1, ds(w * 2, 2)], NC)
                with dve.Fori(start, end, K) as c:
                    dve.reg_add(steps, steps, 1)
                    step = dve.snap(steps, min_val=1, max_val=NC * NW)
                    done = dve.snap(pairs, min_val=0, max_val=NC * NW)
                    dve.wait_ge(ohd_ready, step)
                    v.tensor_tensor(krel, kq[:, ds(c, K), :], nbw[:, ds(w, 1), :].to_broadcast([P, K, 3]), ALU.add).then_inc(krel_ready, 1)
                    dve.wait_ge(krel_ready, step)
                    for k in range(K):
                        dve.wait_ge(pair_used, done + (k + 1))
                        v.tensor_scalar(ohk[:, k, :], tabk, krel[:, k, 0:1], None, ALU.is_equal)
                        v.tensor_scalar(ohs[:, k, 0:P], tabs[:, :], krel[:, k, 1:2], None, ALU.is_equal).then_inc(pair_ready, 1)
                    dve.wait_ge(eaw_used, step + 1)
                    v.tensor_tensor(ohd, tabs[:, 0:W].unsqueeze(1).to_broadcast([P, K, W]),
                                    krel[:, :, 2:3].to_broadcast([P, K, W]), ALU.is_equal).then_inc(ohd_ready, 1)
                    dve.reg_add(pairs, pairs, K)
            dve.wait_ge(window_kept, NW + 2)
            v.tensor_scalar(eaS[:, 0:N], eaS[:, 0:N], 1.0, None, ALU.add).then_inc(eaS_ready, 1)
            dve.wait_ge(indeg_ready, 1)
            link(v.tensor_copy(indeg1, psum[0:P, 5, 0:NB]))
            leave(dve, 2)

            def over_f(a):
                return a.unsqueeze(2).to_broadcast([P, NB, D])

            def over_j(a):
                return a.unsqueeze(1).to_broadcast([P, NB, D])

            roots = [0]

            def std(step):
                step.then_inc(var_ready, 1)
                roots[0] += 1
                dve.wait_ge(std_ready, roots[0])

            def layernorm(x_):
                link(v.tensor_reduce(mean_n, x_, X, ALU.add))
                link(v.tensor_scalar(mean_n, mean_n, 1.0 / D, None, ALU.mult))
                link(v.tensor_tensor(H_, x_, over_f(mean_n), ALU.subtract))
                link(v.tensor_tensor(SQ, H_, H_, ALU.mult))
                link(v.tensor_reduce(var_n, SQ, X, ALU.add))
                std(v.tensor_scalar(var_n, var_n, 1.0 / D, EPS, ALU.mult, ALU.add))
                link(v.reciprocal(tmp_n, tmp_n))
                link(v.scalar_tensor_tensor(out=H_, in0=H_, scalar=0.0, in1=over_f(tmp_n), op0=ALU.max, op1=ALU.mult))

            def split():
                for k in range(3):
                    last = v.tensor_copy(zs[:, :, k, :], H_)
                    if k < 2:
                        link(last)
                        link(v.tensor_tensor(H_, H_, zs[:, :, k, :], ALU.subtract))
                last.then_inc(zs_ready, 1)

            applied = [0]

            def take(per, use):
                base = NB * applied[0]
                applied[0] += 1
                with dve.Fori(0, G) as gg:
                    chain.enter(gg, G * per)
                    for u in range(G):
                        j = gg * G + u
                        dve.wait_ge(y_ready, j + (base + 1))
                        link(v.tensor_reduce(ysum[:, :], bank(u, 3 * D).rearrange("p (k f) -> p f k", k=3), X, ALU.add))
                        use(j)
                        dve.sem_inc(y_free, 1)
                    chain.leave(G)

            def feature_total(step):
                step.then_inc(fsum_ready, 1)
                totals[0] += 1
                dve.wait_ge(fsum_total, totals[0])

            totals = [0]

            def batchnorm(gamma, beta):
                feature_total(v.tensor_reduce(fsum, R_.rearrange("p j f -> p f j"), X, ALU.add))
                link(v.tensor_scalar(scale_f, bank(6, D), 1.0 / N, None, ALU.mult))
                link(v.tensor_tensor(R_, R_, over_j(scale_f), ALU.subtract))
                link(v.tensor_tensor(SQ, R_, R_, ALU.mult))
                feature_total(v.tensor_reduce(fsum, SQ.rearrange("p j f -> p f j"), X, ALU.add))
                std(v.tensor_scalar(fsq, bank(6, D), 1.0 / N, EPS, ALU.mult, ALU.add))
                link(v.reciprocal(tmp_f, tmp_f))
                link(v.tensor_tensor(scale_f, tmp_f, rows[:, gamma, :], ALU.mult))
                link(v.tensor_tensor(R_, R_, over_j(scale_f), ALU.mult))
                link(v.tensor_tensor(R_, R_, over_j(rows[:, beta, :]), ALU.add))
                link(v.tensor_scalar(H_, R_, 0.0, None, ALU.max))

            dve.wait_ge(x_in, 16 * len(LANES))
            layernorm(R_)
            for l in range(3):
                with dve.Fori(0, G) as gg:
                    chain.enter(gg, 5)
                    js = ds(gg * G, G)
                    n = gg + (G * l + 1)
                    link(v.tensor_copy(cat[:, :, 0:D], H_[:, js, :]))
                    v.tensor_tensor(cat[:, :, D:2 * D], H_[:, js, :], indeg1[:, js].unsqueeze(2).to_broadcast([P, G, D]),
                                    ALU.mult).then_inc(cat_ready, 1)
                    dve.wait_ge(z1_ready, n)
                    link(v.tensor_tensor(rz, bank(4, G * D).rearrange("p (i f) -> p i f", i=G), zs[:, js, 0, :], ALU.subtract))
                    link(v.tensor_copy(zs[:, js, 1, :], rz))
                    link(v.tensor_tensor(rz, rz, zs[:, js, 1, :], ALU.subtract))
                    link(v.tensor_copy(zs[:, js, 2, :], rz))
                    v.tensor_copy(R_[:, js, :], bank(5, G * D).rearrange("p (i f) -> p i f", i=G)).then_inc(prod_read, 1)
                    dve.wait_ge(prod_read, n)
                    chain.leave(G)
                dve.sem_inc(zs_ready, 1)
                take(2, lambda j: link(v.tensor_tensor(R_[:, ds(j, 1), :], R_[:, ds(j, 1), :], ysum[:, :].unsqueeze(1), ALU.add)))
                link(v.tensor_scalar(R_, R_, 0.0, None, ALU.max))
                if l < 2:
                    batchnorm(2 * l, 2 * l + 1)
            dve.wait_ge(x_again, 16 * len(LANES))
            link(v.tensor_tensor(X_, X_, R_, ALU.add))
            leave(dve, 3)

            layernorm(X_)
            with dve.Fori(0, G) as gg:
                js = ds(gg * G, G)
                v.tensor_copy(cat[:, :, 0:D], H_[:, js, :]).then_inc(cat_ready, 1)
                dve.wait_ge(prod_ready, gg + (3 * G + 1))
                v.tensor_tensor(R_[:, js, :], bank(4, G * D).rearrange("p (i f) -> p i f", i=G),
                                rows[:, 4, :].unsqueeze(1).to_broadcast([P, G, D]), ALU.add).then_inc(prod_read, 1)
                dve.wait_ge(prod_read, gg + (3 * G + 1))
            dve.sem_inc(rows_ready, 1)
            leave(dve, 4)

            v.memset(zeros_m, 0.0).then_inc(zeros_ready, 1)
            v.memset(ea3w, 0.0).then_inc(zeros_ready, 1)
            with dve.Fori(0, T) as t:
                for u in range(U):
                    dve.wait_ge(gathered[u], t * (16 * G) + 16 * G)
                    dve.wait_ge(ew_ready, t * U + (u + 1))
                    m = msg[0:P, G * u:G * u + G, :]
                    v.tensor_tensor(m, m, bank(4 + u, G * D).rearrange("p (i f) -> p i f", i=G), ALU.add).then_inc(premsg_ready, 1)
                    onehots(t * U + u, u)
            leave(dve, 5)

            hn = psum[0:P, 0:4, :].rearrange("p b k -> p (b k)")[:, 0:BLK].rearrange("p (j f) -> p j f", j=NB)
            with dve.Fori(0, G) as gg:
                chain.enter(gg, 3)
                js = ds(gg * G, G)
                link(v.tensor_copy(cat[:, :, 0:D], H_[:, js, :]))
                v.tensor_copy(cat[:, :, D:2 * D], hn[:, js, :]).then_inc(cat_ready, 1)
                dve.wait_ge(prod_ready, gg + (4 * G + 1))
                link(v.tensor_scalar(R_[:, js, :], bank(6, G * D).rearrange("p (i f) -> p i f", i=G), 0.0, None, ALU.max))
                link(v.tensor_tensor(X_[:, js, :], X_[:, js, :], R_[:, js, :], ALU.add))
                chain.leave(G)
            leave(dve, 6)

            layernorm(X_)
            dve.wait_ge(outdeg_ready, 1)
            link(v.tensor_reduce(norm_out, outdeg4[:, :, :], X, ALU.add))
            link(v.tensor_scalar(norm_in, indeg1, -1.0, 1.0, ALU.add, ALU.max))
            std(v.tensor_scalar(norm_out, norm_out, 1.0, None, ALU.max))
            link(v.reciprocal(norm_in, norm_in))
            link(v.reciprocal(norm_out, norm_out))
            link(v.tensor_tensor(H_, H_, over_f(norm_out), ALU.mult))
            split()
            take(2, lambda j: link(v.scalar_tensor_tensor(out=X_[:, ds(j, 1), :], in0=ysum[:, :].unsqueeze(1),
                                                          scalar=norm_in[:, ds(j, 1)], in1=X_[:, ds(j, 1), :],
                                                          op0=ALU.mult, op1=ALU.add)))
            leave(dve, 7)

            layernorm(X_)
            split()
            take(2, lambda j: link(v.tensor_tensor(X_[:, ds(j, 1), :], X_[:, ds(j, 1), :], ysum[:, :].unsqueeze(1), ALU.add)))
            leave(dve, 8)


_INS = ["x", "src", "dst", "edge_attr_16", "edge_attr_3",
        "L0_gnn_W0", "L0_gnn_b0", "L0_gnn_W1", "L0_gnn_b1", "L0_gnn_W2", "L0_gnn_b2",
        "L0_gnn_g0", "L0_gnn_be0", "L0_gnn_g1", "L0_gnn_be1", "L1_gnn_W1", "L1_gnn_b1", "L1_gnn_W2"]


def kernel(**inputs):
    import numpy as _np
    import concourse.bacc as _bacc
    from concourse import mybir as _mybir
    from concourse.bass_utils import run_bass_kernel_spmd as _run

    nc = _bacc.Bacc("TRN2", target_bir_lowering=False, num_devices=1)
    arrays, args = {}, []
    for name in _INS:
        a = _np.ascontiguousarray(inputs[name])
        arrays[f"in_{name}_dram"] = a
        args.append(nc.dram_tensor(f"in_{name}_dram", a.shape, _mybir.dt.from_np(a.dtype), kind="ExternalInput").ap())
    args.append(nc.dram_tensor("out_0_dram", (N, D), F32, kind="ExternalOutput").ap())
    build(nc, *args)
    r = _run(nc, [arrays], core_ids=[0])
    return r.results[0]["out_0_dram"]
```

```python
from contextlib import ExitStack

import concourse.bass as bass
from concourse import mybir

F32 = mybir.dt.float32
BF16 = mybir.dt.bfloat16
F16 = mybir.dt.float16
I32 = mybir.dt.int32
I16 = mybir.dt.int16
ALU = mybir.AluOpType
ACT = mybir.ActivationFunctionType
X = mybir.AxisListType.X
ds = bass.ds

N, E, D = 3125, 103125, 64
P = 125
NB = N // P
NC = E // P
EF = 16
EX = EF + 1
CT, CP = 15, 55
HALF = 9
W = 20
WP = -(-N // (2 * W))
NW = 2 * WP
WK = W * NB
DP = NW * W
G, U = 5, 3
TURNS = tuple((4 * i, min(4, NB - 4 * i)) for i in range(-(-NB // 4)))
NT = len(TURNS)
HALVES = (slice(0, 13), slice(13, NB))
T = NC // (G * U)
K = 7
KQ = NC + K
KD = 3
EPS = 1e-5
LANES = ((0, 112), (112, P))
SPLIT = ((0, 0, HALF), (1, HALF, CT))


class Chain:

    def __init__(self, engine, sem):
        self.engine, self.sem, self.base, self.t, self.per, self.steps = engine, sem, 0, None, 0, 0

    def link(self, instruction):
        instruction.then_inc(self.sem, 1)
        self.steps += 1
        done = self.base + self.steps
        self.engine.wait_ge(self.sem, done if self.t is None else self.t * self.per + done)

    def start(self, instruction):
        instruction.then_inc(self.sem, 1)
        self.steps += 1
        return self.base + self.steps

    def after(self, count):
        self.engine.wait_ge(self.sem, count)

    def enter(self, t, per):
        self.base, self.t, self.per, self.steps = self.base + self.steps, t, per, 0

    def leave(self, trips):
        assert self.steps == self.per, (self.steps, self.per)
        self.base, self.t, self.steps = self.base + trips * self.per, None, 0


def build(nc, x, src, dst, ea16, ea3, w0, b0, w1, b1, w2, b2, g0, be0, g1, be1, mw1, mb1, mw2, out):
    with ExitStack() as ctx:
        ctx.enter_context(nc.allow_non_contiguous_dma(reason="bias columns"))

        def sb(name, shape, dt):
            return ctx.enter_context(nc.sbuf_tensor(name, shape, dt))

        def sem(name):
            return ctx.enter_context(nc.semaphore(name))

        AT = sb("AT", [P, NB * DP], BF16)
        at3 = AT[:, :].rearrange("p (b d) -> p b d", b=NB)
        dstf = sb("dstf", [P, NC], F32)
        srci = sb("srci", [128, NC + G], I32)
        ident = sb("ident", [128, 128], F32)
        ones = sb("ones", [128, P], F32)
        tabs = sb("tabs", [P, P], F16)
        nbj = sb("nbj", [P, NB], F32)
        Wzy = sb("Wzy", [D, 3, 2, D], F32)
        Wex = sb("Wex", [EX, 3, D], F32)
        W1a = sb("W1a", [D, D], F32)
        W2s = sb("W2s", [128, D], F32)
        rows = sb("rows", [P, 5, D], F32)
        schedj = sb("schedj", [1, NC // G, 2], I16)
        stat = sb("stat", [P, 4, D], F32)
        node = sb("node", [P, 6, NB], F32)
        ysum = sb("ysum", [P, D], F32)
        outdeg4 = sb("outdeg4", [P, NB, 4], F32)
        ARENA = 9720
        arena = sb("arena", [128, ARENA], F32)
        psum = ctx.enter_context(nc.psum_tensor("psum", [128, 8, 512], F32))
        mean_n, var_n, indeg1, norm_in, norm_out, tmp_n = (node[:, i, :] for i in range(6))
        fsum, fsq, scale_f, tmp_f = (stat[:, i, :] for i in range(4))

        def area(at, size, p=P):
            assert at + size <= ARENA, (at, size)
            return arena[0:p, at:at + size]

        BLK = NB * D
        X_ = area(0, BLK).rearrange("p (j f) -> p j f", j=NB)
        H_ = area(BLK, BLK).rearrange("p (j f) -> p j f", j=NB)
        R_ = area(2 * BLK, BLK).rearrange("p (j f) -> p j f", j=NB)
        zs = area(3 * BLK, 3 * BLK // 2).bitcast(BF16).rearrange("p (j k f) -> p j k f", j=NB, k=3)
        SQ = area(3 * BLK, BLK).rearrange("p (j f) -> p j f", j=NB)
        cat_at = 3 * BLK + 3 * BLK // 2
        cat = area(cat_at, 2 * 4 * 128).rearrange("p (h i f) -> p h i f", h=2, f=128)
        catT = area(cat_at + 1024, 2 * 4 * P, 128).rearrange("p (h e) -> p h e", h=2)
        rz = area(cat_at, 2 * 4 * D).rearrange("p (h i f) -> p h i f", h=2, f=D)
        junk = area(cat_at + 512, G * P).bitcast(BF16)
        hT = area(cat_at + 512, 2 * 4 * P, D).rearrange("p (h e) -> p h e", h=2)
        eacT = area(cat_at + 1512, 2 * 4 * P, EX).rearrange("p (h e) -> p h e", h=2)
        kq = area(0, 3 * KQ).rearrange("p (c k) -> p c k", k=3)
        tabk = area(2496, WK // 2).bitcast(F16)
        nbw = area(2746, 3 * NW).rearrange("p (w k) -> p w k", k=3)
        krel = area(9650, 2 * 3 * K).rearrange("p (h c k) -> p h c k", h=2, k=3)
        schedw = area(3242, NW, 1).bitcast(I16)
        zeros = area(3400, 256).bitcast(BF16)
        ohs = area(3656, K * 64).bitcast(BF16).rearrange("p (i d) -> p i d", i=K)
        ohk = area(4104, K * WK // 2).bitcast(BF16).rearrange("p (i d) -> p i d", i=K)
        ohd = area(5854, K * W).rearrange("p (i d) -> p i d", i=K)
        eaw = area(5994, 2 * K * EX).rearrange("p (h i f) -> p h i f", h=2, f=EX)
        dist = area(9400, (K - KD) * P // 2).bitcast(F16).rearrange("p (i d) -> p i d", d=P)
        eaS = area(6240, DP, EX)
        drel = area(3200, U * G).rearrange("p (i d) -> p i d", i=U)
        zeros_m = area(3220, 256).bitcast(BF16)
        oh = area(3810, U * G * P).rearrange("p (i d) -> p i d", i=U * G)
        msg = area(5810, U * G * D, 128).rearrange("p (i f) -> p i f", i=U * G)
        ea3s = area(6770, U * P, 3 * G).rearrange("p (u e) -> p u e", u=U)
        ea3w = area(7895, G * D, 3 * G)
        ring = area(8855, U * G, 128).bitcast(I32)
        zidx = area(8870, G, 128).bitcast(I32)
        TP = CT // 3
        ea3n = area(3656, 2 * TP * 3 * P, CP).rearrange("p (s t e k) -> p s t e k", s=2, t=TP, k=3)
        ea3t = area(3656 + 2 * TP * 3 * P, TP * 3 * P, CP).rearrange("p (t k e) -> p t k e", t=TP, k=3)
        atf = AT[:, :].bitcast(F32)

        def early(at, size, p=P):
            return atf[0:p, at:at + size]

        dnat = early(0, CT * P, CP).bitcast(I32).rearrange("p (t e) -> p t e", t=CT)
        snat = early(1875, CT * P, CP).bitcast(I32).rearrange("p (t e) -> p t e", t=CT)
        dnf = early(3750, CT * P, CP).rearrange("p (t e) -> p t e", t=CT)
        diag = early(5625, 2 * NC, CP).rearrange("p (k t r) -> p k t r", k=2, t=CT)
        m1, m2, m3 = early(7275, NC, WP), early(8100, NC, WP), early(8925, NC, WP)
        up = early(9750, NC, WP)
        down = early(10575, NC, WP)
        qf = early(11400, NC)
        qi = early(12225, NC).bitcast(I32)
        rf = early(13050, NC)
        rng = early(0, 2 * NC, WP).rearrange("p (k c) -> p k c", k=2)
        eaT = early(14000, KQ * EX).rearrange("p (c f) -> p c f", c=KQ)
        eas = early(28150, U * P * EF, CP).rearrange("p (i e f) -> p i e f", i=U, f=EF)
        cmpj = early(38440, CT * (NB - 1), CP).rearrange("p (t j) -> p t j", t=CT)
        jtab = early(34500, NB - 1, CP)
        wlo, whi = early(34530, 2, WP), early(34532, 2, WP)
        dmm = early(34540, 2 * CT, CP).rearrange("p (k t) -> p k t", k=2)
        jmm = early(34570, 2 * CT, CP).rearrange("p (k t) -> p k t", k=2)
        wm = early(34600, 4, WP)
        srcf = early(34700, NC)
        snf = early(36000, CT * P, CP).rearrange("p (t e) -> p t e", t=CT)
        wraw = early(38000, 3 * 145, D).rearrange("p (l f) -> p l f", l=3)

        src_v = src.rearrange("(t r e) -> r t e", t=CT, r=CP)
        dst_v = dst.rearrange("(t r e) -> r t e", t=CT, r=CP)
        ea16_v = ea16.rearrange("(c e) f -> c e f", e=P)
        ea3_v = ea3.rearrange("(t r e) k -> r t (e k)", t=CT, r=CP)
        ea3D = nc.dram_tensor("ea3_by_feature", (NC, 3, P), F32).ap()
        ea3D_v = ea3D.rearrange("(t r) k e -> r t (k e)", t=CT)
        x_v = x.rearrange("(j q) f -> q j f", q=P)
        out_v = out.rearrange("(j q) f -> q j f", q=P)
        eaD = nc.dram_tensor("ea_by_place", (P, KQ, EX), F32).ap()
        eaSD = nc.dram_tensor("ea_sums", (EX, N), F32).ap()
        msgsrc = nc.dram_tensor("msgsrc", (N, D), F32).ap()
        msgsrc_v = msgsrc.rearrange("(j q) f -> q j f", q=P)

        phase_left = sem("phase_left")
        idx_in, w_in, x_in, x_again, ea3w_in = (sem(n) for n in ("idx_in", "w_in", "x_in", "x_again", "ea3w_in"))
        ea_in = [sem(f"ea_in{i}") for i in range(U)]
        ea3_read, ea3_turned, ea3_stored = sem("ea3_read"), sem("ea3_turned"), sem("ea3_stored")
        ea3_in = [sem(f"ea3_in{i}") for i in range(U)]
        gathered = [sem(f"gathered{i}") for i in range(U)]
        drel_ready, krel_ready = sem("drel_ready"), sem("krel_ready")
        dist_ready, src_made = sem("dist_ready"), sem("src_made")
        tables, dve_step, act_step = sem("tables"), sem("dve_step"), sem("act_step")
        idx_f32, idx_T, idx_copied = sem("idx_f32"), sem("idx_T"), sem("idx_copied")
        diag_ready, diag_sum = sem("diag_ready"), sem("diag_sum")
        win_ready, win_T, w_T = sem("win_ready"), sem("win_T"), sem("w_T")
        ea_T, ea_kept, range_copied = sem("ea_T"), sem("ea_kept"), sem("range_copied")
        pads_ready, ea_stored = sem("pads_ready"), sem("ea_stored")
        eaw_in = [sem(f"eaw_in{h}") for h in range(2)]
        ohd_ready, eaw_used, eaS_ready, eaS_stored = sem("ohd_ready"), sem("eaw_used"), sem("eaS_ready"), sem("eaS_stored")
        indeg_ready = sem("indeg_ready")
        eacT_in = [sem(f"eacT_in{h}") for h in range(2)]
        h_ready, turned, hT_ready, zx_ready, zx_read = (sem(n) for n in ("h_ready", "turned", "hT_ready", "zx_ready", "zx_read"))
        oh_ready, oh_used = sem("oh_ready"), sem("oh_used")
        group_used, zeros_ready = sem("group_used"), sem("zeros_ready")
        pair_ready, pair_used, window_done, window_kept = sem("pair_ready"), sem("pair_used"), sem("window_done"), sem("window_kept")
        cat_ready, cat_T, catT_ready = sem("cat_ready"), sem("cat_T"), sem("catT_ready")
        prod_ready, prod_read, z1_ready = sem("prod_ready"), sem("prod_read"), sem("z1_ready")
        y_ready, y_free, zs_ready = sem("y_ready"), sem("y_free"), sem("zs_ready")
        fsum_ready, fsum_total, var_ready, std_ready = sem("fsum_ready"), sem("fsum_total"), sem("var_ready"), sem("std_ready")
        outdeg_ready, rows_ready, rows_out, out_done = sem("outdeg_ready"), sem("rows_ready"), sem("rows_out"), sem("out_done")
        centred, squared, half_ready, rounded = sem("centred"), sem("squared"), sem("half_ready"), sem("rounded")
        ring_ready, ew_ready, premsg_ready, msg_ready = sem("ring_ready"), sem("ew_ready"), sem("premsg_ready"), sem("msg_ready")

        block = ctx.enter_context(nc.Block())
        NTAB = 14
        NWIN = 12 + 2 + 5

        def leave(eng, n):
            eng.drain().then_inc(phase_left, 1)
            eng.wait_ge(phase_left, 5 * n)

        def load_range(eng, pair, at, most):
            eng.load(list(pair), at)
            return eng.snap(pair[0], min_val=0, max_val=most - 1), eng.snap(pair[1], min_val=1, max_val=most)

        def zy(h, nj):
            return psum[0:P, 2 + h, 0:nj * 2 * D].rearrange("p (i k f) -> p i k f", i=nj, k=2)

        def bank(b, cols, p=P):
            return psum[0:p, b, 0:cols]

        @block.sync
        def _(sp):
            sp.dma_start(dnat, dst_v).then_inc(idx_in, 16)
            sp.dma_start(snat, src_v).then_inc(idx_in, 16)
            for l, (w, b) in enumerate(((w0, b0), (w1, b1), (w2, b2))):
                sp.dma_start(wraw[:, l, 0:D], w[:, D:2 * D]).then_inc(w_in, 16)
                sp.dma_start(wraw[:, l, D:2 * D], w[:, 0:D]).then_inc(w_in, 16)
                sp.dma_start(wraw[:, l, 2 * D:2 * D + EF], w[:, 2 * D:2 * D + EF]).then_inc(w_in, 16)
                sp.dma_start(wraw[:, l, 2 * D + EF:2 * D + EX], b.rearrange("(f a) -> f a", a=1)).then_inc(w_in, 16)
            sp.dma_start(W1a[:, :], mw1[0:D, :]).then_inc(w_in, 16)
            sp.dma_start(W2s[:, :], mw2[:, :]).then_inc(w_in, 16)
            for k, r in enumerate((g0, be0, g1, be1, mb1)):
                sp.dma_start(rows[:, k, :], r.rearrange("(a f) -> a f", a=1).to_broadcast([P, D])).then_inc(w_in, 16)
            def load_tile(n, u):
                sp.dma_start(eas[:, u, :, :], ea16_v[ds(n * CP, CP)]).then_inc(ea_in[u], 16)

            def store_tile(n):
                for a, b in LANES:
                    sp.dma_start(eaD[a:b, ds(n * CP, CP), :], eaT[a:b, ds(n * CP, CP), :]).then_inc(ea_stored, 16)

            for u in range(U):
                load_tile(u, u)
            sp.wait_ge(pads_ready, 2)
            for a, b in LANES:
                sp.dma_start(eaD[a:b, NC:KQ, :], eaT[a:b, NC:KQ, :]).then_inc(ea_stored, 16)
            with sp.Fori(0, CT // U - 1) as t:
                for u in range(U):
                    sp.wait_ge(ea_kept, t * U + (u + 1))
                    load_tile(t * U + (u + U), u)
                    store_tile(t * U + u)
            for n in range(CT - U, CT):
                sp.wait_ge(ea_kept, n + 1)
                store_tile(n)
            sp.wait_ge(ea_stored, (CT + 1) * 16 * len(LANES))
            leave(sp, 1)
            steps = ctx.enter_context(sp.register("steps_sp"))
            need = ctx.enter_context(sp.register("need_sp"))
            pair = [ctx.enter_context(sp.register(f"range_sp{i}")) for i in range(2)]
            sp.reg_mov(steps, 0)
            with sp.Fori(0, NW // 2) as t:
                for h in range(2):
                    start, end = load_range(sp, pair, schedw[0:1, ds((t * 2 + h) * 2, 2)], NC)
                    sp.reg_add(need, steps, 1)
                    with sp.Fori(start, end, K) as c:
                        sp.reg_add(steps, steps, 1)
                        sp.wait_ge(eaw_used, sp.snap(need, min_val=1, max_val=NC * NW))
                        sp.reg_add(need, steps, 2)
                        for a, b in LANES:
                            sp.dma_start(eaw[a:b, h, :, :], eaD[a:b, ds(c, K), :]).then_inc(eaw_in[h], 16)
            sp.wait_ge(eaS_ready, 1)
            sp.dma_start(eaSD, eaS[:, 0:N]).then_inc(eaS_stored, 16)
            sp.wait_ge(eaS_stored, 16)
            leave(sp, 2)
            for a, b in LANES:
                sp.dma_start(R_[a:b], x_v[a:b]).then_inc(x_in, 16)
            for a, b in LANES:
                sp.dma_start(X_[a:b], x_v[a:b]).then_inc(x_again, 16)
            for n in range(3 * NT):
                j, nj = TURNS[n % NT]
                if n >= 2:
                    sp.wait_ge(zx_ready, n - 1)
                sp.dma_start(eacT[:, n % 2, 0:nj * P], eaSD[:, j * P:(j + nj) * P]).then_inc(eacT_in[n % 2], 16)
            leave(sp, 3)
            sp.wait_ge(rows_ready, 1)
            for a, b in LANES:
                sp.dma_start(msgsrc_v[a:b], R_[a:b]).then_inc(rows_out, 16)
            sp.wait_ge(rows_out, 16 * len(LANES))
            leave(sp, 4)
            sp.wait_ge(zeros_ready, 2)
            for i in range(G):
                sp.dma_start(ea3w[3 * i:3 * i + 3, i * D:(i + 1) * D], mw1[D:D + 3, :]).then_inc(ea3w_in, 16)
            with sp.Fori(0, T) as t:
                for u in range(U):
                    sp.wait_ge(group_used, t * U + (u + 1))
                    sp.dma_start(ea3s[:, u, :], ea3D[ds((t * U + u) * G, G)].rearrange("i k e -> (i k) e")).then_inc(ea3_in[u], 16)
            for n in range(5, 9):
                leave(sp, n)
            for a, b in LANES:
                sp.dma_start(out_v[a:b], X_[a:b]).then_inc(out_done, 16)
            sp.wait_ge(out_done, 16 * len(LANES))

        @block.gpsimd
        def _(pool):
            g = nc.gpsimd
            loose = dict(allow_small_or_imprecise_dtypes=True)
            g.memset(ident[:, :], 0.0).then_inc(tables, 1)
            g.memset(ones[:, :], 1.0).then_inc(tables, 1)
            g.iota(tabs[:, :], pattern=[[1, P]], base=0, channel_multiplier=0, **loose).then_inc(tables, 1)
            g.iota(nbj[:, :], pattern=[[-P, NB]], base=0, channel_multiplier=0, **loose).then_inc(tables, 1)
            g.iota(tabk, pattern=[[1, NB], [NB, W]], base=0, channel_multiplier=0, **loose).then_inc(tables, 1)
            g.iota(nbw[:, :, 0], pattern=[[-WK, NW]], base=0, channel_multiplier=0, **loose).then_inc(tables, 1)
            g.iota(up, pattern=[[1, NC]], base=1, channel_multiplier=0, **loose).then_inc(tables, 1)
            g.iota(down, pattern=[[-1, NC]], base=NC, channel_multiplier=0, **loose).then_inc(tables, 1)
            g.iota(jtab, pattern=[[P, NB - 1]], base=P, channel_multiplier=0, **loose).then_inc(tables, 1)
            g.iota(wlo, pattern=[[WP * W, 2]], base=0, channel_multiplier=W, **loose).then_inc(tables, 1)
            g.iota(whi, pattern=[[WP * W, 2]], base=W - 1, channel_multiplier=W, **loose).then_inc(tables, 1)
            g.memset(srci[:, :], 0).then_inc(tables, 1)
            g.memset(zeros, 0.0).then_inc(tables, 1)
            pool.wait_ge(tables, 1)
            g.affine_select(out=ident[:, :], in_=ident[:, :], compare_op=ALU.not_equal, fill=1.0, base=0,
                            pattern=[[-1, 128]], channel_multiplier=1).then_inc(tables, 1)
            g.memset(nbw[:, :, 1], 0.0)
            g.iota(nbw[:, :, 2], pattern=[[-W, NW]], base=0, channel_multiplier=0, **loose)
            g.memset(kq[:, NC:KQ, :], -1.0)
            g.memset(eaT[:, :, EF:EX], 1.0).then_inc(pads_ready, 1)
            g.memset(eaT[:, NC:KQ, 0:EF], 0.0).then_inc(pads_ready, 1)
            def read_part(n):
                g.dma_start(ea3n[:, n % 2].rearrange("p t e k -> p t (e k)"), ea3_v[:, n * TP:(n + 1) * TP, :]).then_inc(ea3_read, 16)

            read_part(0)
            for n in range(3):
                pool.wait_ge(ea3_read, 16 * (n + 1))
                if n:
                    pool.wait_ge(ea3_stored, 16 * n)
                if n < 2:
                    read_part(n + 1)
                g.tensor_copy(ea3t, ea3n[:, n % 2].rearrange("p t e k -> p t k e")).then_inc(ea3_turned, 1)
                pool.wait_ge(ea3_turned, n + 1)
                g.dma_start(ea3D_v[:, n * TP:(n + 1) * TP, :], ea3t.rearrange("p t k e -> p t (k e)")).then_inc(ea3_stored, 16)
            pool.wait_ge(ea3_stored, 48)
            leave(pool, 1)
            pair = [ctx.enter_context(pool.register(f"range_pool{i}")) for i in range(2)]
            steps = ctx.enter_context(pool.register("steps_pool"))
            need = ctx.enter_context(pool.register("need_pool"))
            pool.reg_mov(steps, 0)
            with pool.Fori(0, NW // 2) as t:
                for h in range(2):
                    start, end = load_range(pool, pair, schedw[0:1, ds((t * 2 + h) * 2, 2)], NC)
                    pool.reg_add(need, steps, 1)
                    with pool.Fori(start, end, K) as c:
                        pool.reg_add(steps, steps, 1)
                        free = pool.snap(need, min_val=1, max_val=NC * NW)
                        pool.reg_add(need, steps, 2)
                        pool.wait_ge(ohd_ready, free)
                        pool.wait_ge(src_made, free)
                        g.tensor_tensor(krel[:, h], kq[:, ds(c, K), :], nbw[:, ds(t * 2 + h, 1), :].to_broadcast([P, K, 3]),
                                        ALU.add).then_inc(krel_ready, 1)
            for n in range(2, 5):
                leave(pool, n)
            g.memset(zidx, 0).then_inc(ring_ready, 1)
            pool.sem_inc(premsg_ready, U - 1)
            pool.wait_ge(ring_ready, 1)
            g.tensor_tensor(ring[:, 0:G], srci[:, 0:G], zidx, ALU.add).then_inc(ring_ready, 1)
            with pool.Fori(0, T) as t:
                for u in range(U):
                    v = (u + 1) % U
                    pool.wait_ge(premsg_ready, t * U + (u + 1))
                    pool.wait_ge(group_used, t * U + (u + 1))
                    pool.wait_ge(ring_ready, t * U + (u + 2))
                    g.tensor_tensor(ring[:, G * v:G * v + G], srci[:, ds((t * U + (u + 1)) * G, G)], zidx,
                                    ALU.add).then_inc(ring_ready, 1)
                    for i in range(G * u, G * u + G):
                        g.indirect_dma_start(msg[:, i, :], None, msgsrc,
                                             bass.IndirectOffsetOnAxis(ring[:, i:i + 1], 0)).then_inc(gathered[u], 16)
            for n in range(5, 9):
                leave(pool, n)

        @block.scalar
        def _(act):
            a = nc.scalar
            chain = Chain(act, act_step)
            for k, col in enumerate((dstf[:, :], srcf)):
                act.wait_ge(idx_T, k + 1)
                for b, lo, hi in SPLIT:
                    a.copy(col[:, lo * CP:hi * CP], bank(2 * k + b, (hi - lo) * CP)).then_inc(idx_copied, 1)
            act.wait_ge(diag_sum, 1)
            for k in range(2):
                for b, lo, hi in SPLIT:
                    a.copy(rng[:, k, lo * CP:hi * CP], bank(4 + 2 * k + b, (hi - lo) * CP, WP)).then_inc(range_copied, 1)
            with act.Fori(0, CT // U) as t:
                for u in range(U):
                    act.wait_ge(ea_T, t * U + (u + 1))
                    for k in range(2):
                        last = a.copy(eaT[:, ds((t * U + u) * CP, CP), 8 * k:8 * k + 8].rearrange("p c f -> p f c"),
                                      bank(2 * u + k, 8 * CP).rearrange("p (f c) -> p f c", f=8))
                    last.then_inc(ea_kept, 1)
            leave(act, 1)
            act.sem_inc(window_kept, 2)
            pair = [ctx.enter_context(act.register(f"range_act{i}")) for i in range(2)]
            pairs = ctx.enter_context(act.register("pairs_act"))
            steps = ctx.enter_context(act.register("steps_act"))
            act.reg_mov(pairs, 0)
            act.reg_mov(steps, 0)
            act.sem_inc(src_made, 2)

            def sources(w, h):
                start, end = load_range(act, pair, schedw[0:1, ds(w * 2, 2)], NC)
                with act.Fori(start, end, K):
                    act.reg_add(steps, steps, 1)
                    act.reg_add(pairs, pairs, K)
                    step = act.snap(steps, min_val=1, max_val=NC * NW)
                    free = act.snap(pairs, min_val=1, max_val=NC * NW)
                    act.wait_ge(krel_ready, step)
                    act.wait_ge(src_made, step + 1)
                    for k in range(KD, K):
                        last = a.activation(dist[:, k - KD, :], tabs[:, :], ACT.Abs, bias=krel[:, h, k, 1:2], scale=-1.0)
                    last.then_inc(dist_ready, 1)
                    act.wait_ge(dist_ready, step)
                    act.wait_ge(pair_used, free)
                    a.activation(ohs[:, KD:K, 0:P], dist, ACT.Relu, bias=ones[0:P, 0:1], scale=-1.0).then_inc(src_made, 1)

            def keep(w, h):
                act.wait_ge(window_done, w + 1)
                a.copy(at3[:, :, ds(w * W, W)], bank(1 + h, WK).rearrange("p (b d) -> p b d", d=W))
                a.copy(eaS[:, ds(w * W, W)], bank(3 + h, W, EX)).then_inc(window_kept, 1)

            sources(0, 0)
            with act.Fori(0, NW // 2 - 1) as t:
                for h in range(2):
                    sources(t * 2 + (h + 1), 1 - h)
                    keep(t * 2 + h, h)
            sources(NW - 1, 1)
            keep(NW - 2, 0)
            keep(NW - 1, 1)
            leave(act, 2)

            def copy_turned(n):
                nj = TURNS[n % NT][1]
                if n >= 2:
                    act.wait_ge(zx_ready, n - 1)
                act.wait_ge(turned, n + 1)
                a.copy(hT[:, n % 2, 0:nj * P], bank(n % 2, nj * P, D)).then_inc(hT_ready, 1)

            roots = [0]

            def root():
                act.wait_ge(var_ready, roots[0] + 1)
                roots[0] += 1
                return roots[0]

            normed, halves = [0], [0]

            def node_root():
                for js in HALVES:
                    normed[0] += 1
                    act.wait_ge(centred, normed[0])
                    a.activation(SQ[:, js, :], H_[:, js, :], ACT.Square).then_inc(squared, 1)
                root()
                a.activation(tmp_n, var_n, ACT.Sqrt).then_inc(std_ready, 1)
                halves[0] += len(HALVES)

            def round_parts():
                halves[0] -= len(HALVES)
                for k in range(3):
                    for js in HALVES:
                        halves[0] += 1
                        act.wait_ge(half_ready, halves[0])
                        last = a.copy(zs[:, js, k, :], H_[:, js, :])
                        if k < 2:
                            last.then_inc(rounded, 1)
                last.then_inc(zs_ready, 1)

            node_root()
            for l in range(3):
                for g in range(NT + 1):
                    n = NT * l + g
                    if g < NT:
                        copy_turned(n)
                    if g:
                        j, nj = TURNS[g - 1]
                        act.wait_ge(zx_ready, n)
                        a.copy(zs[:, j:j + nj, 0, :], zy((n - 1) % 2, nj)[:, :, 0, :]).then_inc(z1_ready, 1)
                if l == 0:
                    with act.Fori(0, NB) as b:
                        chain.enter(b, 4)
                        for k in range(4):
                            w4 = DP // 4
                            chain.link(a.activation(junk[:, 0:w4], at3[:, ds(b, 1), k * w4:(k + 1) * w4].rearrange("p a d -> p (a d)"),
                                                    ACT.Copy, accum_out=outdeg4[:, ds(b, 1), k:k + 1].rearrange("p a k -> p (a k)")))
                        chain.leave(NB)
                    act.sem_inc(outdeg_ready, 1)
                if l < 2:
                    root()
                    a.activation(tmp_f, fsq, ACT.Sqrt).then_inc(std_ready, 1)
            leave(act, 3)
            node_root()
            for g in range(NT):
                copy_turned(3 * NT + g)
            leave(act, 4)
            root()
            chain.link(a.activation(norm_in, norm_in, ACT.Sqrt))
            a.activation(norm_out, norm_out, ACT.Sqrt).then_inc(std_ready, 1)
            with act.Fori(0, T) as t:
                for u in range(U):
                    act.wait_ge(premsg_ready, t * U + (u + U))
                    m = msg[0:P, G * u:G * u + G, :]
                    a.activation(m, m, ACT.Relu).then_inc(msg_ready, 1)
            leave(act, 5)
            for n, (j, nj) in enumerate(TURNS):
                if n >= 2:
                    act.wait_ge(prod_ready, n - 1)
                act.wait_ge(cat_T, n + 1)
                a.copy(catT[:, n % 2, 0:nj * P], bank(4 + n % 2, nj * P, 128)).then_inc(catT_ready, 1)
            leave(act, 6)
            node_root()
            round_parts()
            leave(act, 7)
            node_root()
            round_parts()
            leave(act, 8)

        @block.tensor
        def _(pe):
            mm, tp = nc.tensor.matmul, nc.tensor.transpose
            pe.wait_ge(tables, NTAB)
            for k, nat in enumerate((dnf, snf)):
                pe.wait_ge(idx_f32, k + 1)
                for b, lo, hi in SPLIT:
                    for t in range(lo, hi):
                        last = tp(psum[0:P, 2 * k + b, (t - lo) * CP:(t - lo + 1) * CP], nat[:, t, :], ident[0:CP, 0:CP])
                last.then_inc(idx_T, 1)
            pe.wait_ge(diag_ready, 1)
            for k in range(2):
                for b, lo, hi in SPLIT:
                    last = mm(bank(4 + 2 * k + b, (hi - lo) * CP, WP), ones[0:CP, 0:WP],
                              diag[:, k, lo:hi, :].rearrange("p t r -> p (t r)"), start=True, stop=True)
            last.then_inc(diag_sum, 1)
            pe.wait_ge(idx_copied, 4)
            pe.wait_ge(range_copied, 4)
            with pe.Fori(0, CT // U) as t:
                for u in range(U):
                    pe.wait_ge(ea_in[u], t * 16 + 16)
                    mm(psum[0:P, 7, 0:1], ones[0:CP, 0:P], ones[0:CP, 0:1], start=True, stop=True)
                    for f in range(EF):
                        last = tp(psum[0:P, 2 * u + f // 8, (f % 8) * CP:(f % 8 + 1) * CP], eas[:, u, :, f], ident[0:CP, 0:CP])
                    last.then_inc(ea_T, 1)
            pe.wait_ge(ea_kept, CT)
            pe.wait_ge(diag_ready, 2)
            for k in range(2):
                for b, lo, hi in SPLIT:
                    last = mm(bank(2 * k + b, (hi - lo) * CP, 1), ones[0:CP, 0:1],
                              diag[:, k, lo:hi, :].rearrange("p t r -> p (t r)"), start=True, stop=True)
            last.then_inc(diag_sum, 1)
            pe.wait_ge(win_ready, 1)
            for k in range(4):
                last = mm(psum[0:1, 4, k * WP:(k + 1) * WP], wm[:, k:k + 1], ident[0:WP, 0:WP], start=True, stop=True)
            last.then_inc(win_T, 1)
            pe.wait_ge(w_in, 16 * NWIN)
            for l in range(3):
                for k in range(2):
                    tp(psum[0:D, 7, (2 * l + k) * D:(2 * l + k + 1) * D], wraw[:, l, k * D:(k + 1) * D], ident[0:D, 0:D])
                last = tp(psum[0:EX, 6, l * D:(l + 1) * D], wraw[:, l, 128:128 + EX], ident[0:D, 0:D])
            last.then_inc(w_T, 1)
            leave(pe, 1)

            pe.sem_inc(oh_used, 2)
            units = ctx.enter_context(pe.register("units_pe"))
            pair = [ctx.enter_context(pe.register(f"range_pe{i}")) for i in range(2)]
            pe.reg_mov(units, 0)

            def scatter_group(grp, u, place, payload):
                lo, end = load_range(pe, pair, schedj[0:1, ds(grp, 1), :].rearrange("p a b -> p (a b)"), NB)
                with pe.Fori(lo, end) as j:
                    pe.reg_add(units, units, 1)
                    pe.wait_ge(oh_ready, pe.snap(units, min_val=1, max_val=2 * NC * NB))
                    for i in range(G):
                        last = mm(place(j), oh[:, G * u + i, :], payload(i), start=False, stop=False, skip_group_check=True)
                    last.then_inc(oh_used, 1)

            def zero(banks, z):
                for b in banks:
                    last = mm(bank(b, 512), z[:, 0:P], z[:, 0:512], start=True, stop=True)
                return last

            pe.sem_inc(pair_used, K)
            pe.sem_inc(eaw_used, 2)
            pairs = ctx.enter_context(pe.register("pairs_pe"))
            steps = ctx.enter_context(pe.register("steps_pe"))
            landed = [ctx.enter_context(pe.register(f"landed_pe{h}")) for h in range(2)]
            for reg in [pairs, steps] + landed:
                pe.reg_mov(reg, 0)
            with pe.Fori(0, NW // 2) as t:
                for h in range(2):
                    start, end = load_range(pe, pair, schedw[0:1, ds((t * 2 + h) * 2, 2)], NC)
                    pe.wait_ge(window_kept, t * 2 + (h + 1))
                    mm(bank(1 + h, WK), zeros[:, 0:P], zeros[:, 0:WK], start=True, stop=True)
                    mm(bank(3 + h, W, EX), zeros[:, 0:EX], zeros[:, 0:W], start=True, stop=True)
                    with pe.Fori(start, end, K):
                        done = pe.snap(pairs, min_val=0, max_val=NC * NW)
                        pe.reg_add(steps, steps, 1)
                        step = pe.snap(steps, min_val=1, max_val=NC * NW)
                        for k in range(K):
                            if k == KD:
                                pe.wait_ge(src_made, step + 2)
                            pe.wait_ge(pair_ready, done + (k + 1))
                            mm(bank(1 + h, WK), ohs[:, k, 0:P], ohk[:, k, :], start=False, stop=False,
                               skip_group_check=True).then_inc(pair_used, 1)
                        pe.reg_add(pairs, pairs, K)
                        pe.reg_add(landed[h], landed[h], 16 * len(LANES))
                        in_place = pe.snap(landed[h], min_val=1, max_val=32 * NC * NW)
                        pe.wait_ge(ohd_ready, step + 2)
                        pe.wait_ge(eaw_in[h], in_place)
                        for k in range(K):
                            last = mm(bank(3 + h, W, EX), eaw[:, h, k, :], ohd[:, k, :], start=False, stop=False,
                                      skip_group_check=True)
                        last.then_inc(eaw_used, 1)
                    mm(bank(1 + h, 1), zeros[:, 0:P], zeros[:, 0:1], start=False, stop=True,
                       skip_group_check=True).then_inc(window_done, 1)
            pe.wait_ge(eaS_ready, 1)
            for j in range(NB):
                last = mm(psum[0:P, 5, j:j + 1], eaS[:, j * P:(j + 1) * P], ident[0:EX, EF:EX], start=True, stop=True)
            last.then_inc(indeg_ready, 1)
            leave(pe, 2)

            def turn_h(n):
                j, nj = TURNS[n % NT]
                if n >= 2:
                    pe.wait_ge(hT_ready, n - 1)
                for i in range(nj):
                    last = tp(psum[0:D, n % 2, i * P:(i + 1) * P], H_[:, j + i, :], ident[0:P, 0:P])
                last.then_inc(turned, 1)

            applied = [0]

            def apply():
                base = NB * applied[0]
                applied[0] += 1
                pe.wait_ge(zs_ready, applied[0])
                with pe.Fori(0, G) as gg:
                    for u in range(G):
                        pe.wait_ge(y_free, gg * G + (base + u + 1))
                        for b in range(NB):
                            last = mm(bank(u, 3 * D), at3[:, b, ds((gg * G + u) * P, P)],
                                      zs[:, b, :, :].rearrange("p k f -> p (k f)"), start=(b == 0), stop=(b == NB - 1))
                        last.then_inc(y_ready, 1)

            totals = [0]

            def total():
                totals[0] += 1
                pe.wait_ge(fsum_ready, totals[0])
                mm(bank(6, D), ones[0:P, 0:P], fsum, start=True, stop=True).then_inc(fsum_total, 1)

            pe.sem_inc(y_free, G)
            for l in range(3):
                pe.wait_ge(h_ready, l + 1)
                for g in range(NT + 1):
                    n = NT * l + g
                    if g < NT:
                        turn_h(n)
                    if g:
                        j, nj = TURNS[g - 1]
                        h = (n - 1) % 2
                        pe.wait_ge(hT_ready, n)
                        if n > 2:
                            pe.wait_ge(zx_read, n - 2)
                        for i in range(nj):
                            mm(psum[0:P, 2 + h, i * 2 * D:(i + 1) * 2 * D], hT[:, h, i * P:(i + 1) * P],
                               Wzy[:, l, :, :].rearrange("p k f -> p (k f)"), start=True, stop=True)
                        pe.wait_ge(eacT_in[h], 16 * ((n - 1) // 2 + 1))
                        for i in range(nj):
                            last = mm(psum[0:P, 4 + h, i * D:(i + 1) * D], eacT[:, h, i * P:(i + 1) * P], Wex[:, l, :],
                                      start=True, stop=True)
                        last.then_inc(zx_ready, 1)
                apply()
                if l < 2:
                    total()
                    total()
            leave(pe, 3)
            pe.wait_ge(h_ready, 4)
            for g in range(NT + 1):
                n = 3 * NT + g
                if g < NT:
                    turn_h(n)
                if g:
                    h = (n - 1) % 2
                    pe.wait_ge(hT_ready, n)
                    pe.wait_ge(zx_read, n - 2)
                    for i in range(TURNS[g - 1][1]):
                        last = mm(psum[0:P, 2 + h, i * D:(i + 1) * D], hT[:, h, i * P:(i + 1) * P], W1a[:, :], start=True, stop=True)
                    last.then_inc(zx_ready, 1)
            leave(pe, 4)
            pe.wait_ge(zeros_ready, 2)
            zero(range(4), zeros_m)
            pe.sem_inc(group_used, U)
            pe.wait_ge(ea3w_in, 16 * G)

            def edges_part(t, u):
                pe.wait_ge(ea3_in[u], t * 16 + 16)
                mm(bank(4 + u, G * D), ea3s[:, u, :], ea3w, start=True, stop=True).then_inc(ew_ready, 1)

            def sum_messages(t, u):
                pe.wait_ge(msg_ready, t * U + (u + 1))
                scatter_group(t * U + u, u, lambda j: psum[0:P, 0:4, :].rearrange("p b k -> p (b k)")[:, ds(j * D, D)],
                              lambda i: msg[0:P, G * u + i, :])
                mm(psum[0:P, 7, 0:1], zeros_m[:, 0:P], zeros_m[:, 0:1], start=True, stop=True).then_inc(group_used, 1)

            edges_part(0, 0)
            with pe.Fori(0, T - 1) as t:
                for u in range(U):
                    edges_part(t + (u + 1) // U, (u + 1) % U)
                    sum_messages(t, u)
            for u in range(U):
                if u + 1 < U:
                    edges_part(T - 1, u + 1)
                sum_messages(T - 1, u)
            leave(pe, 5)
            for n in range(NT + 1):
                if n < NT:
                    pe.wait_ge(cat_ready, n + 1)
                    if n >= 2:
                        pe.wait_ge(catT_ready, n - 1)
                    for i in range(TURNS[n][1]):
                        last = tp(psum[:, 4 + n % 2, i * P:(i + 1) * P], cat[:, n % 2, i, :], ident[0:P, 0:P])
                    last.then_inc(cat_T, 1)
                if n:
                    h = (n - 1) % 2
                    pe.wait_ge(catT_ready, n)
                    if n > 2:
                        pe.wait_ge(prod_read, n - 2)
                    for i in range(TURNS[n - 1][1]):
                        last = mm(psum[0:P, 6 + h, i * D:(i + 1) * D], catT[:, h, i * P:(i + 1) * P], W2s[:, :], start=True, stop=True)
                    last.then_inc(prod_ready, 1)
            leave(pe, 6)
            apply()
            leave(pe, 7)
            apply()
            leave(pe, 8)

        @block.vector
        def _(dve):
            v = nc.vector
            chain = Chain(dve, dve_step)
            link = chain.link
            dve.wait_ge(idx_in, 32)
            v.tensor_copy(dnf, dnat).then_inc(idx_f32, 1)
            v.tensor_copy(snf, snat).then_inc(idx_f32, 1)
            dve.wait_ge(idx_f32, 1)
            dve.wait_ge(tables, NTAB)
            link(v.tensor_reduce(dmm[:, 0, :], dnf, X, ALU.min))
            link(v.tensor_reduce(dmm[:, 1, :], dnf, X, ALU.max))
            rr = ident[0:CP, 0:CP].unsqueeze(1).to_broadcast([CP, CT, CP])

            def diagonal(vals):
                for k in range(2):
                    link(v.tensor_tensor(diag[:, k, :, :], rr, vals[:, k, :].unsqueeze(2).to_broadcast([CP, CT, CP]), ALU.mult))

            diagonal(dmm)
            dve.sem_inc(diag_ready, 1)
            for k in range(2):
                link(v.tensor_tensor(cmpj, dmm[:, k, :].unsqueeze(2).to_broadcast([CP, CT, NB - 1]),
                                     jtab.unsqueeze(1).to_broadcast([CP, CT, NB - 1]), ALU.is_ge))
                link(v.tensor_reduce(jmm[:, k, :], cmpj, X, ALU.add))
            link(v.tensor_scalar(jmm[:, 1, :], jmm[:, 1, :], 1.0, None, ALU.add))
            dve.wait_ge(diag_sum, 1)
            diagonal(jmm)
            dve.sem_inc(diag_ready, 1)
            dve.wait_ge(idx_copied, 4)
            v.tensor_copy(srci[0:P, 0:NC], srcf)
            link(v.tensor_scalar(qi, srcf, 1.0 / P, -0.5 + 0.5 / P, ALU.mult, ALU.add))
            link(v.tensor_copy(qf, qi))
            link(v.scalar_tensor_tensor(out=rf, in0=qf, scalar=-float(P), in1=srcf, op0=ALU.mult, op1=ALU.add))
            link(v.scalar_tensor_tensor(out=qf, in0=rf, scalar=float(P), in1=qf, op0=ALU.is_ge, op1=ALU.add))
            link(v.tensor_scalar(rf, rf, 0.0, None, ALU.is_lt))
            link(v.tensor_tensor(qf, qf, rf, ALU.subtract))
            link(v.scalar_tensor_tensor(out=kq[:, 0:NC, 1], in0=qf, scalar=-float(P), in1=srcf, op0=ALU.mult, op1=ALU.add))
            link(v.tensor_copy(kq[:, 0:NC, 2], dstf[:, :]))
            link(v.scalar_tensor_tensor(out=kq[:, 0:NC, 0], in0=dstf[:, :], scalar=float(NB), in1=qf, op0=ALU.mult, op1=ALU.add))
            dve.wait_ge(range_copied, 4)
            for h in range(2):
                ws, we = (wm[:, 2 * h + k:2 * h + k + 1] for k in range(2))
                link(v.tensor_scalar(m1, rng[:, 0, :], whi[:, h:h + 1], None, ALU.is_le))
                link(v.scalar_tensor_tensor(out=m2, in0=rng[:, 1, :], scalar=wlo[:, h:h + 1], in1=m1, op0=ALU.is_ge, op1=ALU.mult))
                link(v.tensor_tensor(m3, m2, up, ALU.mult))
                link(v.tensor_reduce(we, m3, X, ALU.max))
                link(v.tensor_tensor(m3, m2, down, ALU.mult))
                link(v.tensor_reduce(ws, m3, X, ALU.max))
                link(v.tensor_scalar(we, we, 1.0, None, ALU.max))
                link(v.tensor_scalar(ws, ws, -1.0, float(NC), ALU.mult, ALU.add))
                link(v.scalar_tensor_tensor(out=ws, in0=we, scalar=-1.0,
                                            in1=ws, op0=ALU.add, op1=ALU.min))
            dve.sem_inc(win_ready, 1)
            dve.wait_ge(diag_sum, 2)
            for k, op in enumerate((ALU.min, ALU.max)):
                for b, lo, hi in SPLIT:
                    last = v.tensor_reduce(schedj[:, lo * CP // G:hi * CP // G, k:k + 1].rearrange("p c a -> p (c a)"),
                                           bank(2 * k + b, (hi - lo) * CP, 1).rearrange("p (g i) -> p g i", i=G), X, op)
            dve.wait_ge(win_T, 1)
            for h in range(2):
                for k in range(2):
                    last = v.tensor_copy(schedw[:, 2 * h * WP:2 * (h + 1) * WP].rearrange("p (w k) -> p w k", k=2)[:, :, k],
                                         psum[0:1, 4, (2 * h + k) * WP:(2 * h + k + 1) * WP])
            dve.wait_ge(w_T, 1)
            link(v.tensor_copy(Wzy[:, :, :, :], psum[0:D, 7, 0:6 * D].rearrange("p (l k f) -> p l k f", l=3, k=2)))
            link(v.tensor_copy(Wex[:, :, :], psum[0:EX, 6, 0:3 * D].rearrange("p (l f) -> p l f", l=3)))
            leave(dve, 1)

            units = ctx.enter_context(dve.register("units_dve"))
            need = ctx.enter_context(dve.register("need_dve"))
            pair = [ctx.enter_context(dve.register(f"range_dve{i}")) for i in range(2)]
            dve.reg_mov(units, 0)

            def onehots(grp, u):
                lo, end = load_range(dve, pair, schedj[0:1, ds(grp, 1), :].rearrange("p a b -> p (a b)"), NB)
                dve.reg_add(need, units, 1)
                with dve.Fori(lo, end) as j:
                    dve.reg_add(units, units, 1)
                    unit = dve.snap(units, min_val=1, max_val=2 * NC * NB)
                    dve.wait_ge(oh_used, dve.snap(need, min_val=1, max_val=2 * NC * NB))
                    dve.reg_add(need, units, 2)
                    v.tensor_scalar(drel[:, u, :], dstf[:, ds(grp * G, G)], nbj[:, ds(j, 1)], None, ALU.add).then_inc(drel_ready, 1)
                    dve.wait_ge(drel_ready, unit)
                    v.tensor_tensor(oh[:, G * u:G * u + G, :], tabs[:, :].unsqueeze(1).to_broadcast([P, G, P]),
                                    drel[:, u, :].unsqueeze(2).to_broadcast([P, G, P]), ALU.is_equal).then_inc(oh_ready, 1)

            pairs = ctx.enter_context(dve.register("pairs_dve"))
            steps = ctx.enter_context(dve.register("steps_dve"))
            dve.reg_mov(pairs, 0)
            dve.reg_mov(steps, 0)
            dve.sem_inc(ohd_ready, 2)
            with dve.Fori(0, NW // 2) as t:
                for h in range(2):
                    start, end = load_range(dve, pair, schedw[0:1, ds((t * 2 + h) * 2, 2)], NC)
                    with dve.Fori(start, end, K):
                        dve.reg_add(steps, steps, 1)
                        step = dve.snap(steps, min_val=1, max_val=NC * NW)
                        done = dve.snap(pairs, min_val=0, max_val=NC * NW)
                        dve.wait_ge(krel_ready, step)
                        for k in range(K):
                            dve.wait_ge(pair_used, done + (k + 1))
                            last = v.tensor_scalar(ohk[:, k, :], tabk, krel[:, h, k, 0:1], None, ALU.is_equal)
                            if k < KD:
                                last = v.tensor_scalar(ohs[:, k, 0:P], tabs[:, :], krel[:, h, k, 1:2], None, ALU.is_equal)
                            last.then_inc(pair_ready, 1)
                        dve.wait_ge(eaw_used, step + 1)
                        v.tensor_tensor(ohd, tabs[:, 0:W].unsqueeze(1).to_broadcast([P, K, W]),
                                        krel[:, h, :, 2:3].to_broadcast([P, K, W]), ALU.is_equal).then_inc(ohd_ready, 1)
                        dve.reg_add(pairs, pairs, K)
            dve.wait_ge(window_kept, NW + 2)
            v.tensor_scalar(eaS[:, 0:N], eaS[:, 0:N], 1.0, None, ALU.add).then_inc(eaS_ready, 1)
            dve.wait_ge(indeg_ready, 1)
            link(v.tensor_copy(indeg1, psum[0:P, 5, 0:NB]))
            leave(dve, 2)

            def over_f(a, js):
                return a[:, js].unsqueeze(2).to_broadcast([P, js.stop - js.start, D])

            def over_j(a):
                return a.unsqueeze(1).to_broadcast([P, NB, D])

            roots = [0]

            def std(step):
                step.then_inc(var_ready, 1)
                roots[0] += 1
                dve.wait_ge(std_ready, roots[0])

            normed, rounds = [0], [0]

            def layernorm(x_, outer=None):
                for js in HALVES:
                    last = chain.start(v.tensor_reduce(mean_n[:, js], x_[:, js, :], X, ALU.add))
                chain.after(last)
                link(v.tensor_scalar(mean_n, mean_n, 1.0 / D, None, ALU.mult))
                for js in HALVES:
                    v.tensor_tensor(H_[:, js, :], x_[:, js, :], over_f(mean_n, js), ALU.subtract).then_inc(centred, 1)
                for js in HALVES:
                    normed[0] += 1
                    dve.wait_ge(squared, normed[0])
                    last = chain.start(v.tensor_reduce(var_n[:, js], SQ[:, js, :], X, ALU.add))
                chain.after(last)
                std(v.tensor_scalar(var_n, var_n, 1.0 / D, EPS, ALU.mult, ALU.add))
                link(v.reciprocal(tmp_n, tmp_n))
                if outer is not None:
                    link(v.tensor_tensor(tmp_n, tmp_n, outer, ALU.mult))
                for js in HALVES:
                    v.scalar_tensor_tensor(out=H_[:, js, :], in0=H_[:, js, :], scalar=0.0, in1=over_f(tmp_n, js),
                                           op0=ALU.max, op1=ALU.mult).then_inc(half_ready, 1)

            def split():
                for k in range(2):
                    for js in HALVES:
                        rounds[0] += 1
                        dve.wait_ge(rounded, rounds[0])
                        v.tensor_tensor(H_[:, js, :], H_[:, js, :], zs[:, js, k, :], ALU.subtract).then_inc(half_ready, 1)

            applied = [0]

            def take(per, use):
                base = NB * applied[0]
                applied[0] += 1
                with dve.Fori(0, G) as gg:
                    chain.enter(gg, G * per)
                    for u in range(G):
                        j = gg * G + u
                        dve.wait_ge(y_ready, j + (base + 1))
                        link(v.tensor_reduce(ysum[:, :], bank(u, 3 * D).rearrange("p (k f) -> p f k", k=3), X, ALU.add))
                        use(j)
                        dve.sem_inc(y_free, 1)
                    chain.leave(G)

            def feature_total(step):
                step.then_inc(fsum_ready, 1)
                totals[0] += 1
                dve.wait_ge(fsum_total, totals[0])

            totals = [0]

            def batchnorm(gamma, beta):
                feature_total(v.tensor_reduce(fsum, R_.rearrange("p j f -> p f j"), X, ALU.add))
                link(v.tensor_scalar(scale_f, bank(6, D), 1.0 / N, None, ALU.mult))
                link(v.tensor_tensor(R_, R_, over_j(scale_f), ALU.subtract))
                link(v.tensor_tensor(SQ, R_, R_, ALU.mult))
                feature_total(v.tensor_reduce(fsum, SQ.rearrange("p j f -> p f j"), X, ALU.add))
                std(v.tensor_scalar(fsq, bank(6, D), 1.0 / N, EPS, ALU.mult, ALU.add))
                link(v.reciprocal(tmp_f, tmp_f))
                link(v.tensor_tensor(scale_f, tmp_f, rows[:, gamma, :], ALU.mult))
                link(v.tensor_tensor(R_, R_, over_j(scale_f), ALU.mult))
                link(v.tensor_tensor(R_, R_, over_j(rows[:, beta, :]), ALU.add))
                link(v.tensor_scalar(H_, R_, 0.0, None, ALU.max))

            dve.wait_ge(x_in, 16 * len(LANES))
            layernorm(R_)
            for l in range(3):
                if l == 0:
                    dve.wait_ge(half_ready, len(HALVES))
                dve.sem_inc(h_ready, 1)
                for g, (j, nj) in enumerate(TURNS):
                    n = NT * l + g
                    js, h = slice(j, j + nj), n % 2
                    deg = indeg1[:, js].unsqueeze(2).to_broadcast([P, nj, D])
                    rest, zy_ = rz[:, h, 0:nj, :], zy(h, nj)
                    dve.wait_ge(z1_ready, n + 1)
                    a1 = chain.start(v.tensor_tensor(rest, zy_[:, :, 0, :], zs[:, js, 0, :], ALU.subtract))
                    b1_ = chain.start(v.tensor_tensor(R_[:, js, :], zy_[:, :, 1, :], deg, ALU.mult))
                    chain.after(a1)
                    a2 = chain.start(v.tensor_copy(zs[:, js, 1, :], rest))
                    chain.after(b1_)
                    b2_ = chain.start(v.tensor_tensor(R_[:, js, :], R_[:, js, :], zy_[:, :, 0, :], ALU.add))
                    chain.after(a2)
                    a3 = chain.start(v.tensor_tensor(rest, rest, zs[:, js, 1, :], ALU.subtract))
                    chain.after(b2_)
                    v.tensor_tensor(R_[:, js, :], R_[:, js, :], bank(4 + h, nj * D).rearrange("p (i f) -> p i f", i=nj),
                                    ALU.add).then_inc(zx_read, 1)
                    chain.after(a3)
                    a4 = chain.start(v.tensor_copy(zs[:, js, 2, :], rest))
                chain.after(a4)
                dve.wait_ge(zx_read, NT * (l + 1))
                dve.sem_inc(zs_ready, 1)
                take(2, lambda j: link(v.tensor_tensor(R_[:, ds(j, 1), :], R_[:, ds(j, 1), :], ysum[:, :].unsqueeze(1), ALU.add)))
                link(v.tensor_scalar(R_, R_, 0.0, None, ALU.max))
                if l < 2:
                    batchnorm(2 * l, 2 * l + 1)
            dve.wait_ge(x_again, 16 * len(LANES))
            link(v.tensor_tensor(X_, X_, R_, ALU.add))
            leave(dve, 3)

            layernorm(X_)
            dve.wait_ge(half_ready, 2 * len(HALVES))
            dve.sem_inc(h_ready, 1)
            for g, (j, nj) in enumerate(TURNS):
                n = 3 * NT + g
                dve.wait_ge(zx_ready, n + 1)
                v.tensor_tensor(R_[:, j:j + nj, :], bank(2 + n % 2, nj * D).rearrange("p (i f) -> p i f", i=nj),
                                rows[:, 4, :].unsqueeze(1).to_broadcast([P, nj, D]), ALU.add).then_inc(zx_read, 1)
            dve.wait_ge(zx_read, 4 * NT)
            dve.sem_inc(rows_ready, 1)
            leave(dve, 4)

            v.memset(zeros_m, 0.0).then_inc(zeros_ready, 1)
            v.memset(ea3w, 0.0).then_inc(zeros_ready, 1)
            dve.wait_ge(outdeg_ready, 1)
            link(v.tensor_reduce(norm_out, outdeg4[:, :, :], X, ALU.add))
            link(v.tensor_scalar(norm_in, indeg1, -1.0, 1.0, ALU.add, ALU.max))
            std(v.tensor_scalar(norm_out, norm_out, 1.0, None, ALU.max))
            link(v.reciprocal(norm_in, norm_in))
            link(v.reciprocal(norm_out, norm_out))
            with dve.Fori(0, T) as t:
                for u in range(U):
                    dve.wait_ge(gathered[u], t * (16 * G) + 16 * G)
                    dve.wait_ge(ew_ready, t * U + (u + 1))
                    m = msg[0:P, G * u:G * u + G, :]
                    v.tensor_tensor(m, m, bank(4 + u, G * D).rearrange("p (i f) -> p i f", i=G), ALU.add).then_inc(premsg_ready, 1)
                    onehots(t * U + u, u)
            leave(dve, 5)

            hn = psum[0:P, 0:4, :].rearrange("p b k -> p (b k)")[:, 0:BLK].rearrange("p (j f) -> p j f", j=NB)
            for n in range(NT + 1):
                if n < NT:
                    j, nj = TURNS[n]
                    if n >= 2:
                        dve.wait_ge(cat_T, n - 1)
                    v.tensor_copy(cat[:, n % 2, 0:nj, 0:D], H_[:, j:j + nj, :])
                    v.tensor_copy(cat[:, n % 2, 0:nj, D:2 * D], hn[:, j:j + nj, :]).then_inc(cat_ready, 1)
                if n:
                    j, nj = TURNS[n - 1]
                    dve.wait_ge(prod_ready, n)
                    v.scalar_tensor_tensor(out=X_[:, j:j + nj, :], in0=bank(6 + (n - 1) % 2, nj * D).rearrange("p (i f) -> p i f", i=nj),
                                           scalar=0.0, in1=X_[:, j:j + nj, :], op0=ALU.max, op1=ALU.add).then_inc(prod_read, 1)
            dve.wait_ge(prod_read, NT)
            leave(dve, 6)

            layernorm(X_, norm_out)
            split()
            take(2, lambda j: link(v.scalar_tensor_tensor(out=X_[:, ds(j, 1), :], in0=ysum[:, :].unsqueeze(1),
                                                          scalar=norm_in[:, ds(j, 1)], in1=X_[:, ds(j, 1), :],
                                                          op0=ALU.mult, op1=ALU.add)))
            leave(dve, 7)

            layernorm(X_)
            split()
            take(2, lambda j: link(v.tensor_tensor(X_[:, ds(j, 1), :], X_[:, ds(j, 1), :], ysum[:, :].unsqueeze(1), ALU.add)))
            leave(dve, 8)


_INS = ["x", "src", "dst", "edge_attr_16", "edge_attr_3",
        "L0_gnn_W0", "L0_gnn_b0", "L0_gnn_W1", "L0_gnn_b1", "L0_gnn_W2", "L0_gnn_b2",
        "L0_gnn_g0", "L0_gnn_be0", "L0_gnn_g1", "L0_gnn_be1", "L1_gnn_W1", "L1_gnn_b1", "L1_gnn_W2"]


def kernel(**inputs):
    import numpy as _np
    import concourse.bacc as _bacc
    from concourse import mybir as _mybir
    from concourse.bass_utils import run_bass_kernel_spmd as _run

    nc = _bacc.Bacc("TRN2", target_bir_lowering=False, num_devices=1)
    arrays, args = {}, []
    for name in _INS:
        a = _np.ascontiguousarray(inputs[name])
        arrays[f"in_{name}_dram"] = a
        args.append(nc.dram_tensor(f"in_{name}_dram", a.shape, _mybir.dt.from_np(a.dtype), kind="ExternalInput").ap())
    args.append(nc.dram_tensor("out_0_dram", (N, D), F32, kind="ExternalOutput").ap())
    build(nc, *args)
    r = _run(nc, [arrays], core_ids=[0])
    return r.results[0]["out_0_dram"]
```
